# Optimizing a Trainium2 kernel written in Bass

```python
import numpy as np
import jax
import jax.numpy as jnp

def _softmax(x, axis=-1):
    return jax.nn.softmax(x, axis=axis)

def _gelu(x):
    return jax.nn.gelu(x, approximate=True)

def _silu(x):
    return jax.nn.silu(x)

def _sigmoid(x):
    return jax.nn.sigmoid(x)

def _layernorm(x, axis=-1, eps=1e-05):
    m = jnp.mean(x, axis=axis, keepdims=True)
    v = jnp.var(x, axis=axis, keepdims=True)
    return (x - m) / jnp.sqrt(v + eps)

def _scatter_add(tgt, idx, src, axis=0):
    return tgt.at[idx].add(src)

def _segment_sum(src, seg, n):
    return jax.ops.segment_sum(src, seg, n)
kernel_name = 'mk_prb_d1_jaxref_r4_5739b7'

def setup_inputs(seed: int=0):
    np.random.seed(seed)
    _w = jnp.asarray

    def _L0_attn_setup():
        import jax, jax.numpy as jnp
        import numpy as np
        NUM_HEADS = 16
        key = jax.random.key(seed)
        k1, k2, k3 = jax.random.split(key, 3)
        B, D, N = (2, 512, 256)
        x = jax.random.normal(k1, (B, D, N), dtype=jnp.float32)
        W_qkv = jax.random.normal(k2, (N, 3 * N), dtype=jnp.float32) * (1.0 / np.sqrt(N))
        b_qkv = jax.random.normal(k3, (3 * N,), dtype=jnp.float32) * 0.01
        return {'x': x, 'W_qkv': W_qkv, 'b_qkv': b_qkv}
    _L0_attn_in = _L0_attn_setup()

    def _L0_ffn_setup():
        import jax, jax.numpy as jnp
        import numpy as np
        D_MODEL = 256
        EXPANSION = 4
        D_HIDDEN = D_MODEL * EXPANSION
        NUM_STAGES = int(np.log2(D_HIDDEN))

        def butterfly(y, weights, dim):
            lead = y.shape[:-1]
            for stage in range(weights.shape[0]):
                s = 2 ** stage
                nb = dim // (2 * s)
                yr = y.reshape(*lead, nb, 2, s)
                a = yr[..., 0, :]
                b = yr[..., 1, :]
                w = weights[stage].reshape(nb, s, 2, 2)
                na = w[..., 0, 0] * a + w[..., 0, 1] * b
                nb2 = w[..., 1, 0] * a + w[..., 1, 1] * b
                y = jnp.stack([na, nb2], axis=-2).reshape(*lead, dim)
            return y
        key = jax.random.key(seed)
        ks = jax.random.split(key, 6)
        B, S = (4, 512)
        x = jax.random.normal(ks[0], (B, S, D_MODEL), jnp.float32)
        W_exp = jax.random.normal(ks[1], (D_MODEL, D_HIDDEN), jnp.float32) * 0.02
        b_exp = jnp.zeros((D_HIDDEN,), jnp.float32)
        up_weights = jax.random.normal(ks[2], (NUM_STAGES, D_HIDDEN // 2, 2, 2), jnp.float32) * 0.02
        up_bias = jnp.zeros((D_HIDDEN,), jnp.float32)
        down_weights = jax.random.normal(ks[3], (NUM_STAGES, D_HIDDEN // 2, 2, 2), jnp.float32) * 0.02
        W_con = jax.random.normal(ks[4], (D_HIDDEN, D_MODEL), jnp.float32) * 0.02
        b_con = jnp.zeros((D_MODEL,), jnp.float32)
        down_bias = jnp.zeros((D_MODEL,), jnp.float32)
        return dict(x=x, W_exp=W_exp, b_exp=b_exp, up_weights=up_weights, up_bias=up_bias, down_weights=down_weights, W_con=W_con, b_con=b_con, down_bias=down_bias)
    _L0_ffn_in = _L0_ffn_setup()
    _d = {'L0_attn_x': _L0_attn_in['x'], 'L0_attn_W_qkv': _L0_attn_in['W_qkv'], 'L0_attn_b_qkv': _L0_attn_in['b_qkv'], 'L0_ffn_W_exp': _L0_ffn_in['W_exp'], 'L0_ffn_b_exp': _L0_ffn_in['b_exp'], 'L0_ffn_up_weights': _L0_ffn_in['up_weights'], 'L0_ffn_up_bias': _L0_ffn_in['up_bias'], 'L0_ffn_down_weights': _L0_ffn_in['down_weights'], 'L0_ffn_W_con': _L0_ffn_in['W_con'], 'L0_ffn_b_con': _L0_ffn_in['b_con'], 'L0_ffn_down_bias': _L0_ffn_in['down_bias']}
    _x0 = _d['L0_attn_x']
    _d['L0_attn_x'] = jax.random.normal(jax.random.fold_in(jax.random.key(seed), 1), (2, 4096, 256), dtype=_x0.dtype)
    del _x0
    return _d

def reference(L0_attn_x, L0_attn_W_qkv, L0_attn_b_qkv, L0_ffn_W_exp, L0_ffn_b_exp, L0_ffn_up_weights, L0_ffn_up_bias, L0_ffn_down_weights, L0_ffn_W_con, L0_ffn_b_con, L0_ffn_down_bias):

    def _L0_attn_ref(x, W_qkv, b_qkv):
        import jax, jax.numpy as jnp
        import numpy as np
        NUM_HEADS = 16
        B, D, N = x.shape
        H = NUM_HEADS
        p = N // H
        qkv = (x @ W_qkv + b_qkv).reshape(B, D, 3, H, p).transpose(2, 0, 3, 1, 4)
        q, k, v = (qkv[0], qkv[1], qkv[2])
        scores = jax.nn.softmax(jnp.einsum('bhip,bhjp->bhij', q, k), axis=-1)
        out = jnp.einsum('bhij,bhjp->bhip', scores, v)
        return out.reshape(B, D, N)

    def _L0_ffn_ref(x, W_exp, b_exp, up_weights, up_bias, down_weights, W_con, b_con, down_bias):
        import jax, jax.numpy as jnp
        import numpy as np
        D_MODEL = 256
        EXPANSION = 4
        D_HIDDEN = D_MODEL * EXPANSION
        NUM_STAGES = int(np.log2(D_HIDDEN))

        def butterfly(y, weights, dim):
            lead = y.shape[:-1]
            for stage in range(weights.shape[0]):
                s = 2 ** stage
                nb = dim // (2 * s)
                yr = y.reshape(*lead, nb, 2, s)
                a = yr[..., 0, :]
                b = yr[..., 1, :]
                w = weights[stage].reshape(nb, s, 2, 2)
                na = w[..., 0, 0] * a + w[..., 0, 1] * b
                nb2 = w[..., 1, 0] * a + w[..., 1, 1] * b
                y = jnp.stack([na, nb2], axis=-2).reshape(*lead, dim)
            return y
        h = jnp.einsum('bsd,dh->bsh', x, W_exp) + b_exp
        h = butterfly(h, up_weights, D_HIDDEN)
        h = jax.nn.gelu(h + up_bias, approximate=False)
        h = butterfly(h, down_weights, D_HIDDEN)
        y = jnp.einsum('bsh,hd->bsd', h, W_con) + b_con
        return y + down_bias
    x = L0_attn_x
    xn = _layernorm(x, axis=-1)
    x = x + _L0_attn_ref(xn, L0_attn_W_qkv, L0_attn_b_qkv) + _L0_ffn_ref(xn, L0_ffn_W_exp, L0_ffn_b_exp, L0_ffn_up_weights, L0_ffn_up_bias, L0_ffn_down_weights, L0_ffn_W_con, L0_ffn_b_con, L0_ffn_down_bias)
    return x

_drawn_inputs = setup_inputs


def setup_inputs(seed=0):
    import zlib

    import numpy as np

    out = dict(_drawn_inputs(seed))
    spreads = {'L0_ffn_b_exp': (0.0, 0.1),
     'L0_ffn_up_bias': (0.0, 0.1),
     'L0_ffn_b_con': (0.0, 0.1),
     'L0_ffn_down_bias': (0.0, 0.1)}
    factors = {'L0_attn_b_qkv': 4.322}
    for name, (base, spread) in spreads.items():
        noise = np.random.default_rng([zlib.crc32(name.encode()), seed]).standard_normal(out[name].shape)
        drawn = base * np.exp(spread * noise) if base else spread * noise
        out[name] = jnp.asarray(drawn.astype(out[name].dtype))
    for name, factor in factors.items():
        out[name] = (out[name] * factor).astype(out[name].dtype)
    return out
```

```python
from contextlib import ExitStack

import concourse.bass as bass
from concourse import mybir

F32 = mybir.dt.float32
BF16 = mybir.dt.bfloat16
ALU = mybir.AluOpType
ACT = mybir.ActivationFunctionType
AX_X = mybir.AxisListType.X

P = 128
BANK = 512
EPS = 1e-5
HEADS = 16


class Chain:

    def __init__(self, engine, sem, done=0):
        self.engine, self.sem, self.done = engine, sem, done

    def __call__(self, instruction):
        self.done = self.done + 1
        instruction.then_inc(self.sem, 1)
        self.engine.wait_ge(self.sem, self.done)


def attention_and_butterfly_ffn(nc, x, w_qkv, b_qk_columns, b_v, w_exp, b_exp, up_planes, up_bias_columns, down_planes,
                                w_con_t, b_con, down_bias, out):
    B, N, D = x.shape
    HD = D // HEADS
    KD = D // P
    TILES = B * N // P
    CT = BANK // P
    CHUNKS = TILES // CT
    HID = w_exp.shape[1]
    HT = HID // P
    STAGES = up_planes.shape[0]
    PAIRS = HID // 2
    QB = 2048
    SUPER = B * N * HEADS // QB
    QG = QB // BANK
    QT = QB // P
    KT = N // P
    PARTS = 3
    ROWS = 6 * HD
    VW = 32
    REGIONS = QT * N // (2 * BANK)
    M_KTS = 27

    q_dram = nc.dram_tensor("q_parts", [PARTS, B * D, N], BF16, kind="Internal").ap()
    k_dram = nc.dram_tensor("k_parts", [PARTS, B * D, N], BF16, kind="Internal").ap()
    v_dram = nc.dram_tensor("v_columns", [B * HEADS, P, KT, HD], F32, kind="Internal").ap()
    xnt_dram = nc.dram_tensor("xn_transposed", [P, KD, B * N], F32, kind="Internal").ap()

    x_tiles = x.rearrange("b (t p) d -> p (b t) d", p=P)
    out_tiles = out.rearrange("b (t p) d -> p (b t) d", p=P)

    with ExitStack() as ctx:
        def sb(name, shape, dt=F32):
            return ctx.enter_context(nc.sbuf_tensor(name, shape, dt))

        def sem(name):
            return ctx.enter_context(nc.semaphore(name))

        psum = ctx.enter_context(nc.psum_tensor("psum", [P, 8, BANK], F32))
        y = sb("y", [P, TILES, D])
        ident = sb("ident", [P, P])
        ident_bf = sb("ident_bf", [P, P], BF16)
        one = sb("one", [1, 2])
        w_up = sb("w_up", [P, 3, HID])
        w_down_t = sb("w_down_t", [P, KD, HID])
        planes = sb("planes", [P, 2, 4, PAIRS])
        fold = sb("fold", [P, 3, 3, PAIRS])

        arena = sb("arena", [P, 18432])
        at = [0]

        def take(shape, dt=F32):
            words = 1
            for n in shape[1:]:
                words *= n
            if dt == BF16:
                words //= 2
            ap = arena[0:shape[0], at[0]:at[0] + words]
            at[0] += words
            assert at[0] <= 18432
            if dt == BF16:
                ap = ap.bitcast(BF16)
            if len(shape) == 3:
                ap = ap.rearrange("p (a b) -> p a b", b=shape[2])
            if len(shape) == 4:
                ap = ap.rearrange("p (a b c) -> p a b c", b=shape[2], c=shape[3])
            return ap

        def row(vector, n=P):
            return vector.rearrange("(a d) -> a d", a=1).to_broadcast([n, vector.shape[0]])

        wqkv = take([P, KD, 3 * D])
        bqk = take([P, 2 * KD])
        bv = take([P, D])
        btail = take([P, 2, D])
        stats = take([P, 2 * CT, 6])
        mv = take([P, 2 * CT, 2])
        std = take([P, 2, CT])
        rstd = take([P, 2, CT])
        eps = take([P, 1])
        wait_slot = take([P, 1])
        xn = take([P, 2 * CT, D])
        xnt = take([P, 2 * KD, BANK])
        full = take([P, 2 * KD, BANK])
        rest = take([P, 2, BANK])
        v_sb = take([P, 2 * HEADS, CT * HD])
        parts = take([P, 2 * KD * PARTS, BANK], BF16)

        ps_xt, ps_qk, ps_v = psum[:, 0:2, :], psum[:, 2:6, :], psum[:, 6:8, :]

        s_w = sem("weights_loaded")
        s_ident = sem("ident_made")
        s_x = [sem(f"x_loaded{n}") for n in range(2)]
        s_moments = sem("moments_done")
        s_std = sem("std_done")
        s_rstd = sem("rstd_done")
        s_xn = sem("xn_done")
        s_res = sem("residual_bias_added")
        s_xt_ps = sem("xt_transposed")
        s_xt = sem("xt_copied")
        s_qk_ps = sem("qk_multiplied")
        s_full = sem("qk_full_copied")
        s_high = sem("high_part_done")
        s_parts = sem("parts_done")
        s_v_ps = sem("v_multiplied")
        s_v = sem("v_done")
        s_dve = sem("dve_chain1")
        s_parts_out = [sem(f"parts_stored{n}") for n in range(2 * KD)]
        s_v_out = [sem(f"v_stored{n}") for n in range(2)]
        s_xt_out = [sem(f"xt_stored{n}") for n in range(2)]

        def chunk_loop(engine, step, head=0):
            with engine.Fori(0, CHUNKS // 2 - 2) as i:
                for p in range(2):
                    step(2 * i + p, i, p, CHUNKS)
            for c in range(CHUNKS - 4, CHUNKS):
                step(c, c // 2, c % 2, CHUNKS - c)

        with nc.Block() as block:
            @block.gpsimd
            def _(pool):
                nc.gpsimd.memset(ident[:, :], 0.0).then_inc(s_ident, 1)
                nc.gpsimd.memset(ident_bf[:, :], 0.0).then_inc(s_ident, 1)
                nc.gpsimd.memset(one[:, :], 1.0).then_inc(s_ident, 1)
                nc.gpsimd.memset(eps, EPS).then_inc(s_ident, 1)
                pool.wait_ge(s_ident, 4)
                for m in (ident, ident_bf):
                    nc.gpsimd.affine_select(out=m[:, :], in_=m[:, :], compare_op=ALU.not_equal, fill=1.0,
                                            base=0, pattern=[[-1, P]], channel_multiplier=1).then_inc(s_ident, 1)
                pool.wait_ge(s_w, 16 * 5)
                nc.gpsimd.tensor_tensor(btail[:, 0, :], btail[:, 0, :], btail[:, 1, :], ALU.add).then_inc(s_res, 1)
                pool.wait_ge(s_res, 1)
                tail_bias = btail[:, 0, :].unsqueeze(1).to_broadcast([P, CT, D])
                with pool.Fori(0, CHUNKS) as c:
                    pool.wait_ge(s_xn, CT * c + CT)
                    tiles = y[:, bass.ds(CT * c, CT), :]
                    nc.gpsimd.tensor_tensor(tiles, tiles, tail_bias, ALU.add).then_inc(s_res, 1)

            @block.sync
            def _(sp):
                sp.dma_start(y[:, 0:CT, :], x_tiles[:, 0:CT, :]).then_inc(s_x[0], 16)
                sp.dma_start(y[:, CT:2 * CT, :], x_tiles[:, CT:2 * CT, :]).then_inc(s_x[1], 16)
                sp.dma_start(wqkv, w_qkv.rearrange("(k p) n -> p k n", p=P)).then_inc(s_w, 16)
                sp.dma_start(bqk, b_qk_columns).then_inc(s_w, 16)
                sp.dma_start(bv, row(b_v)).then_inc(s_w, 16)
                sp.dma_start(btail[:, 0, :], row(b_con)).then_inc(s_w, 16)
                sp.dma_start(btail[:, 1, :], row(down_bias)).then_inc(s_w, 16)
                for c in range(2, 4):
                    sp.wait_ge(s_moments, 2 * CT * (c - 1))
                    sp.dma_start(y[:, CT * c:CT * c + CT, :], x_tiles[:, CT * c:CT * c + CT, :]).then_inc(s_x[c % 2], 16)

                def step(c, i, p, left):
                    if left > 4:
                        sp.wait_ge(s_moments, 2 * CT * (c + 3))
                        sp.dma_start(y[:, bass.ds(CT * c + 4 * CT, CT), :],
                                     x_tiles[:, bass.ds(CT * c + 4 * CT, CT), :]).then_inc(s_x[p], 16)
                    b, of_row = c // (CHUNKS // B), c % (CHUNKS // B)
                    sp.wait_ge(s_xt, KD * c + KD)
                    sp.dma_start(xnt_dram[:, :, bass.ds(BANK * c, BANK)], xnt[:, KD * p:KD * p + KD, :]).then_inc(s_xt_out[p], 16)
                    for m in range(2 * KD):
                        sp.wait_ge(s_parts, 2 * KD * c + m + 1)
                        rows = bass.ds(D * b + P * (m % KD), P)
                        dst = (q_dram if m < KD else k_dram)[:, rows, bass.ds(BANK * of_row, BANK)]
                        sp.dma_start(dst.rearrange("n r k -> r n k"), parts[:, PARTS * m:PARTS * m + PARTS, :])\
                          .then_inc(s_parts_out[m], 16)
                    sp.wait_ge(s_v, 2 * c + 2)
                    dst = v_dram[bass.ds(HEADS * b, HEADS), :, bass.ds(CT * of_row, CT), :].rearrange("h p t d -> p h (t d)")
                    sp.dma_start(dst, v_sb[:, HEADS * p:HEADS * p + HEADS, :]).then_inc(s_v_out[p], 16)

                chunk_loop(sp, step)
                for m in range(2 * KD):
                    sp.wait_ge(s_parts_out[m], 16 * CHUNKS)
                for p in range(2):
                    sp.wait_ge(s_v_out[p], 16 * CHUNKS // 2)
                    sp.wait_ge(s_xt_out[p], 16 * CHUNKS // 2)

            @block.scalar
            def _(act):
                def deviation(c, p):
                    act.wait_ge(s_moments, 2 * CT * c + 2 * CT)
                    nc.scalar.activation(std[:, p, :], mv[:, CT * p:CT * p + CT, 1], ACT.Sqrt, bias=eps).then_inc(s_std, 1)

                act.wait_ge(s_ident, 6)
                deviation(0, 0)
                deviation(1, 1)
                act.wait_ge(s_xt_ps, 1)
                for k in range(KD):
                    nc.scalar.copy(xnt[:, k, :], ps_xt[:, k, :]).then_inc(s_xt, 1)
                act.wait_ge(s_w, 16 * 5)

                def step(c, i, p, left):
                    if left > 1:
                        q = 1 - p
                        act.wait_ge(s_xt_ps, c + 2)
                        act.wait_ge(s_xt_out[q], 16 * (i + p))
                        act.wait_ge(s_v_ps, 2 * c)
                        for k in range(KD):
                            nc.scalar.copy(xnt[:, KD * q + k, :], ps_xt[:, k, :]).then_inc(s_xt, 1)
                    for m in range(2 * KD):
                        act.wait_ge(s_qk_ps, 2 * KD * c + m + 1)
                        act.wait_ge(s_parts, 2 * KD * c)
                        dst, src = full[:, m, :], ps_qk[:, m, :]
                        if m < KD:
                            dst = dst.rearrange("p (t k) -> p k t", t=QT)
                            src = src.rearrange("p (k t) -> p k t", t=QT)
                        nc.scalar.activation(dst, src, ACT.Identity, bias=bqk[:, m:m + 1]).then_inc(s_full, 1)
                        act.wait_ge(s_full, 2 * KD * c + m + 1)
                        act.wait_ge(s_parts_out[m], 16 * c)
                        nc.scalar.copy(parts[:, PARTS * m, :], full[:, m, :]).then_inc(s_high, 1)
                    if left > 2:
                        deviation(c + 2, p)

                chunk_loop(act, step)

            @block.vector
            def _(dve):
                def x_tile(c, t):
                    return y[:, bass.ds(CT * c + t, 1), :].rearrange("p o d -> p (o d)")

                def moments(c, i, p, again=True):
                    dve.wait_ge(s_x[p], 16 * i + 16)
                    if again:
                        dve.wait_ge(s_xn, CT * c - CT)
                    for t in range(CT):
                        nc.vector.bn_stats(stats[:, CT * p + t, :], x_tile(c, t)).then_inc(s_moments, 1)
                    dve.wait_ge(s_moments, 2 * CT * c + CT)
                    nc.vector.memset(wait_slot, 0.0)
                    for t in range(CT):
                        nc.vector.bn_aggr(mv[:, CT * p + t, :], stats[:, CT * p + t, :]).then_inc(s_moments, 1)

                def normalise(c, p, again=True):
                    dve.wait_ge(s_std, c + 1)
                    if again:
                        dve.wait_ge(s_xt_ps, c - 1)
                    nc.vector.reciprocal(rstd[:, p, :], std[:, p, :]).then_inc(s_rstd, 1)
                    dve.wait_ge(s_rstd, c + 1)
                    for t in range(CT):
                        nc.vector.tensor_scalar(xn[:, CT * p + t, :], x_tile(c, t), mv[:, CT * p + t, 0:1],
                                                rstd[:, p, t:t + 1], ALU.subtract, ALU.mult).then_inc(s_xn, 1)

                for c in range(2):
                    moments(c, 0, c, again=False)
                    normalise(c, c, again=False)
                dve.wait_ge(s_w, 16 * 5)
                bv_pair = bv.unsqueeze(1).to_broadcast([P, 2, D]).rearrange("p t (h d) -> p t h d", d=HD)

                def split(c, m):
                    dve.wait_ge(s_high, 2 * KD * c + m + 1)
                    chain = Chain(dve, s_dve, 2 * (2 * KD * c + m))
                    r = rest[:, m % 2, :]
                    chain(nc.vector.tensor_tensor(r, full[:, m, :], parts[:, PARTS * m, :], ALU.subtract))
                    chain(nc.vector.tensor_copy(parts[:, PARTS * m + 1, :], r))
                    nc.vector.tensor_tensor(parts[:, PARTS * m + 2, :], r, parts[:, PARTS * m + 1, :], ALU.subtract)\
                      .then_inc(s_parts, 1)

                def step(c, i, p, left):
                    if left > 2:
                        moments(c + 2, i + 1, p)
                    for m in range(2):
                        split(c, m)
                    if left > 2:
                        normalise(c + 2, p)
                    for m in range(2, 2 * KD):
                        split(c, m)
                    dve.wait_ge(s_v_out[p], 16 * i)
                    for t in range(2):
                        dve.wait_ge(s_v_ps, 2 * c + t + 1)
                        dst = v_sb[:, HEADS * p:HEADS * p + HEADS, 2 * HD * t:2 * HD * t + 2 * HD]
                        nc.vector.tensor_tensor(dst.rearrange("p h (t d) -> p t h d", d=HD),
                                                ps_v[:, t, :].rearrange("p (t h d) -> p t h d", t=2, d=HD), bv_pair, ALU.add)\
                          .then_inc(s_v, 1)

                chunk_loop(dve, step)

            @block.tensor
            def _(pe):
                def transposes(c, p):
                    pe.wait_ge(s_xn, CT * c + CT)
                    pe.wait_ge(s_xt, KD * c)
                    for k in range(KD):
                        for t in range(CT):
                            last = nc.tensor.transpose(ps_xt[:, k, P * t:P * t + P],
                                                       xn[:, CT * p + t, P * k:P * k + P], ident[:, :])
                    last.then_inc(s_xt_ps, 1)

                pe.wait_ge(s_ident, 6)
                transposes(0, 0)
                pe.wait_ge(s_w, 16 * 5)

                def step(c, i, p, left):
                    if left > 1:
                        transposes(c + 1, 1 - p)
                    pe.wait_ge(s_xt, KD * c + KD)
                    pe.wait_ge(s_full, 2 * KD * c)
                    for m in range(2 * KD):
                        for k in range(KD):
                            last = nc.tensor.matmul(ps_qk[:, m, :], wqkv[:, k, P * m:P * m + P],
                                                    xnt[:, KD * p + k, :], start=(k == 0), stop=(k == KD - 1))
                        last.then_inc(s_qk_ps, 1)
                    pe.wait_ge(s_v, 2 * c)
                    for t in range(CT):
                        for k in range(KD):
                            last = nc.tensor.matmul(ps_v[:, t // 2, (t % 2) * D:(t % 2) * D + D],
                                                    xnt[:, KD * p + k, P * t:P * t + P],
                                                    wqkv[:, k, 2 * D:3 * D], start=(k == 0), stop=(k == KD - 1))
                        if t % 2:
                            last.then_inc(s_v_ps, 1)

                chunk_loop(pe, step)

        at[0] = 0
        k_rows = take([P, 2, N], BF16)
        q_rows = take([P, 4, QB], BF16)
        probs = take([P, 4, QG * BANK])
        v_cols = take([P, 2 * KT, VW])
        o_t = sb("o_t", [P, QT, VW])
        maxima = sb("maxima", [P, REGIONS])
        neg_max = sb("neg_max", [P, 3, QT])
        neg_parts = sb("neg_parts", [P, P], BF16)
        neg_rows = sb("neg_rows", [PARTS * QT, P], BF16)
        recip = sb("recip", [P, QT])

        ps_max = [psum[:, 0:2, :], psum[:, 2:4, :]]
        ps_s = psum[:, 4:6, :]
        ps_o = psum[:, 6:8, :]
        ps_neg = psum[:, 0, 0:P // 2].bitcast(BF16)

        s_q = [sem(f"q_rows_loaded{n}") for n in range(4)]
        s_k = [sem(f"k_rows_loaded{n}") for n in range(2)]
        s_vc = [sem(f"v_cols_loaded{n}") for n in range(2)]
        s_set = sem("constants_set")
        s_region = sem("region_multiplied")
        s_region_free = sem("region_free")
        s_neg_ps = sem("neg_parts_transposed")
        s_neg_rows = sem("neg_rows_copied")
        s_neg_in = sem("neg_rows_in_place")
        s_score = sem("scores_multiplied")
        s_exp = sem("exps_done")
        s_pv = sem("probs_used")
        s_o_free = sem("o_banks_free")
        s_fin = sem("maxima_finished")
        s_evac = sem("sums_taken")
        s_plane = [sem(f"planes_loaded{n}") for n in range(2)]
        s_wld = sem("ffn_weights_loaded")
        s_fold = sem("pool_chain")
        LOADS = 3
        FIN = 6
        EVAC = 3

        def pairs_loop(engine, step):
            with engine.Fori(0, B) as b:
                with engine.Fori(0, HEADS // 2) as j:
                    for c in range(4):
                        i = b * (HEADS // 2) + j
                        step(4 * i + c, c, i, b, 2 * j + c // 2)

        with nc.Block() as block:
            @block.gpsimd
            def _(pool):
                ones = Chain(pool, s_set)
                ones(nc.gpsimd.memset(k_rows[ROWS:ROWS + PARTS, :, :], 1.0))
                ones(nc.gpsimd.memset(v_cols[:, :, HD:HD + 1], 1.0))
                ones(nc.gpsimd.memset(neg_parts[:, PARTS * QT:P], 0.0))
                ones(nc.gpsimd.memset(v_cols[:, :, HD + 1:VW], 0.0))
                chain = Chain(pool, s_fold)
                chain(nc.gpsimd.memset(w_up[:, 2, :], 0.0))
                pool.dma_start(w_up[:, 0:KD, :], w_exp.rearrange("(k p) n -> p k n", p=P)).then_inc(s_wld, 16)
                pool.dma_start(w_up[0:1, 2, :], row(b_exp, 1)).then_inc(s_wld, 16)
                pool.dma_start(w_down_t[:, :, :], w_con_t.rearrange("(k p) n -> p k n", p=P)).then_inc(s_wld, 16)
                pool.wait_ge(s_wld, 48)
                turns = [(w_up, 3, up_planes, s) for s in range(STAGES)]
                turns += [(w_down_t, KD, down_planes, s) for s in reversed(range(STAGES))]

                def load_planes(n):
                    _, _, src, s = turns[n]
                    flat = src[s].rearrange("a b k -> (a b k)")
                    pool.dma_start(planes[:, n % 2, :, :].rearrange("p a k -> p (a k)"), row(flat)).then_inc(s_plane[n % 2], 16)

                load_planes(0)
                for n, (w, rows, _, s) in enumerate(turns):
                    if n + 1 < len(turns):
                        load_planes(n + 1)
                    pool.wait_ge(s_plane[n % 2], 16 * (n // 2 + 1))
                    stride = 2 ** s
                    pair = w[:, :, :].rearrange("p r (n two s) -> p r n two s", two=2, s=stride)
                    down = w is w_down_t
                    for r in range(rows):
                        a, b = pair[:, r, :, 0, :], pair[:, r, :, 1, :]

                        def plane(to, of):
                            index = 2 * of + to if down else 2 * to + of
                            return planes[:, n % 2, index, :].rearrange("p (n s) -> p n s", s=stride)

                        def tmp(q):
                            return fold[:, r, q, :].rearrange("p (n s) -> p n s", s=stride)

                        mult, add = ALU.mult, ALU.add
                        nc.gpsimd.tensor_tensor(tmp(0), a, plane(0, 0), mult).then_inc(s_fold, 1)
                        nc.gpsimd.tensor_tensor(tmp(1), b, plane(0, 1), mult).then_inc(s_fold, 1)
                        chain.done += 2
                        chain(nc.gpsimd.tensor_tensor(tmp(2), a, plane(1, 0), mult))
                        chain(nc.gpsimd.tensor_tensor(a, tmp(0), tmp(1), add))
                        chain(nc.gpsimd.tensor_tensor(tmp(0), b, plane(1, 1), mult))
                        chain(nc.gpsimd.tensor_tensor(b, tmp(2), tmp(0), add))

            @block.sync
            def _(sp):
                def load_q(head, half, slot):
                    for first, part, copies in ((0, 0, 3), (3, 1, 2), (5, 2, 1)):
                        src = q_dram[part:part + 1, bass.ds(HD * head, HD), QB * half:QB * half + QB].to_broadcast([copies, HD, QB])
                        sp.dma_start(q_rows[HD * first:HD * (first + copies), slot, :], src).then_inc(s_q[slot], 16)

                def load_k(head, slot):
                    for first, count in ((0, 3), (3, 2), (5, 1)):
                        src = k_dram[0:count, bass.ds(HD * head, HD), :]
                        sp.dma_start(k_rows[HD * first:HD * (first + count), slot, :], src).then_inc(s_k[slot], 16)

                def load_v(n, slot):
                    src = v_dram[bass.ds(n, 1), :, :, :].rearrange("o p t d -> (o p) t d")
                    sp.dma_start(v_cols[:, KT * slot:KT * slot + KT, 0:HD], src).then_inc(s_vc[slot], 16)

                def place_neg(n, slot):
                    sp.wait_ge(s_neg_rows, n + 1)
                    for r in range(PARTS):
                        dst = q_rows[ROWS + r:ROWS + r + 1, slot, :].rearrange("o (t c) -> o t c", c=P)
                        sp.dma_start(dst, neg_rows[QT * r:QT * r + QT, :]).then_inc(s_neg_in, 16)

                load_k(0, 0)
                load_q(0, 0, 0)
                load_v(0, 0)
                load_q(0, 1, 1)
                place_neg(0, 0)

                def pair(i, last=False):
                    for c in range(4):
                        s = 4 * i + c
                        sp.wait_ge(s_score, KT * QG * s)
                        ahead = -2 * i if last and c >= 2 else c // 2 + 1
                        if not (last and c == 3):
                            load_q(2 * i + ahead, c % 2, (c + 2) % 4)
                        if c % 2 == 0:
                            load_k(2 * i + ahead, (c // 2 + 1) % 2)
                            sp.wait_ge(s_pv, KT * s + 4)
                            load_v(2 * i + ahead, (c // 2 + 1) % 2)
                        if not (last and c == 3):
                            place_neg(s + 1, (c + 1) % 4)

                with sp.Fori(0, SUPER // 4 - 1) as i:
                    pair(i)
                pair(SUPER // 4 - 1, last=True)
                sp.wait_ge(s_neg_in, 16 * PARTS * SUPER)
                for n in range(4):
                    sp.wait_ge(s_q[n], 16 * LOADS * (SUPER // 4 + (n == 0)))
                for n in range(2):
                    sp.wait_ge(s_k[n], 16 * LOADS * (SUPER // 4 + (n == 0)))
                    sp.wait_ge(s_vc[n], 16 * (SUPER // 4 + (n == 0)))

            @block.scalar
            def _(act):
                def step(s, c, i, b, h):
                    for kt in range(KT):
                        act.wait_ge(s_pv, KT * s + kt + 1)
                        for g in range(QG):
                            act.wait_ge(s_score, QG * (KT * s + kt) + g + 1)
                            nc.scalar.activation(probs[:, kt % 4, BANK * g:BANK * g + BANK], ps_s[:, g % 2, :],
                                                 ACT.Exp).then_inc(s_exp, 1)

                pairs_loop(act, step)

            @block.vector
            def _(dve):
                for n, (signal, count) in enumerate(((s_region_free, 2), (s_exp, 2), (s_pv, 4), (s_o_free, 2))):
                    nc.vector.memset(recip[:, n:n + 1], 0.0).then_inc(signal, count)

                def reduce_region(s, r):
                    dve.wait_ge(s_region, REGIONS * s + r + 1)
                    nc.vector.tensor_reduce(maxima[:, r:r + 1], ps_max[r % 2].rearrange("p a b -> p (a b)"), axis=AX_X, op=ALU.max)\
                      .then_inc(s_region_free, 1)

                def finish_maxima(s):
                    dve.wait_ge(s_region_free, REGIONS * s + REGIONS + 2)
                    chain = Chain(dve, s_fin, FIN * s)
                    h, m, l = (neg_parts[:, QT * n:QT * n + QT] for n in range(PARTS))
                    chain(nc.vector.tensor_reduce(neg_max[:, 0, :], maxima[:, :].rearrange("p (t r) -> p t r", t=QT),
                                                  axis=AX_X, op=ALU.max, negate=True))
                    chain(nc.vector.tensor_copy(h, neg_max[:, 0, :]))
                    chain(nc.vector.tensor_tensor(neg_max[:, 1, :], neg_max[:, 0, :], h, ALU.subtract))
                    chain(nc.vector.tensor_copy(m, neg_max[:, 1, :]))
                    chain(nc.vector.tensor_tensor(neg_max[:, 2, :], neg_max[:, 1, :], m, ALU.subtract))
                    nc.vector.tensor_copy(l, neg_max[:, 2, :]).then_inc(s_fin, 1)
                    dve.wait_ge(s_neg_ps, s + 1)
                    dve.wait_ge(s_neg_in, 16 * PARTS * s)
                    nc.vector.tensor_copy(neg_rows[:, :], ps_neg[0:PARTS * QT, :]).then_inc(s_neg_rows, 1)

                def take_sums(s, c, b, h):
                    chain = Chain(dve, s_evac, EVAC * s)
                    dve.wait_ge(s_pv, KT * s + KT + 4)
                    nc.vector.transpose(o_t[:, :, :].rearrange("p t v -> p (t v)"), ps_o[:, c % 2, :]).then_inc(s_o_free, 1)
                    dve.wait_ge(s_o_free, s + 3)
                    chain(nc.vector.reciprocal(recip[:, :], o_t[:, :, HD]))
                    dims = o_t[:, :, 0:HD]
                    chain(nc.vector.tensor_tensor(dims, dims, recip[:, :].unsqueeze(2).to_broadcast([P, QT, HD]), ALU.mult))
                    dst = y[:, bass.ds(b * KT + 2 * h + c % 2, 1), :].rearrange("p o (t d) -> p (o t) d", d=HD)
                    chain(nc.vector.tensor_tensor(dst, dst, dims, ALU.add))

                for r in range(REGIONS):
                    reduce_region(0, r)
                finish_maxima(0)

                def step(s, c, i, b, h):
                    for r in range(REGIONS):
                        reduce_region(s + 1, r)
                    finish_maxima(s + 1)
                    if c > 0:
                        take_sums(s - 1, c - 1, b, h - (1 if c == 2 else 0))
                    if c == 3:
                        take_sums(s, c, b, h)

                pairs_loop(dve, step)

            @block.tensor
            def _(pe):
                def region(s, q_slot, k_slot, r):
                    pe.wait_ge(s_region_free, REGIONS * s + r + 1)
                    for n in range(2):
                        keys = ((r % 4) * 2 + n) * BANK
                        last = nc.tensor.matmul(ps_max[r % 2][:, n, :], q_rows[0:ROWS, q_slot, P * (r // 4):P * (r // 4) + P],
                                                k_rows[0:ROWS, k_slot, keys:keys + BANK], start=True, stop=True)
                    last.then_inc(s_region, 1)

                def transpose_neg(s):
                    pe.wait_ge(s_fin, FIN * (s + 1))
                    nc.tensor.transpose(ps_neg, neg_parts[:, :], ident_bf[:, :]).then_inc(s_neg_ps, 1)

                def sums(s, c, kt):
                    if kt == 0:
                        pe.wait_ge(s_o_free, s + 1)
                    pe.wait_ge(s_exp, QG * (KT * s + kt + 1) + 2)
                    for g in range(QG):
                        last = nc.tensor.matmul(ps_o[VW * g:VW * g + VW, c % 2, :], v_cols[:, KT * (c // 2) + kt, :],
                                                probs[:, kt % 4, BANK * g:BANK * g + BANK],
                                                start=(kt == 0), stop=(kt == KT - 1))
                    last.then_inc(s_pv, 1)

                pe.wait_ge(s_set, 4)
                pe.wait_ge(s_k[0], 16 * LOADS)
                pe.wait_ge(s_q[0], 16 * LOADS)
                for r in range(REGIONS):
                    region(0, 0, 0, r)
                transpose_neg(0)

                def step(s, c, i, b, h):
                    nq, nk = (c + 1) % 4, ((c + 1) // 2) % 2
                    later = i + 1 if c == 3 else i
                    r = 0
                    for kt in range(KT):
                        if kt == 0:
                            pe.wait_ge(s_neg_rows, s + 1)
                            pe.wait_ge(s_q[nq], 16 * LOADS * (later + 1))
                            pe.wait_ge(s_k[nk], 16 * LOADS * (later + 1))
                            pe.wait_ge(s_vc[c // 2], 16 * (i + 1))
                            pe.wait_ge(s_neg_in, 16 * PARTS * (s + 1))
                        upto = min(REGIONS, REGIONS * (kt + 1) // M_KTS)
                        for g in range(QG):
                            pe.wait_ge(s_exp, QG * (KT * s + kt) + g + 1)
                            nc.tensor.matmul(ps_s[:, g % 2, :], k_rows[0:ROWS + PARTS, c // 2, P * kt:P * kt + P],
                                             q_rows[0:ROWS + PARTS, c, BANK * g:BANK * g + BANK],
                                             start=True, stop=True).then_inc(s_score, 1)
                            if g == 2 and kt > 0:
                                sums(s, c, kt - 1)
                            elif r < upto:
                                region(s + 1, nq, nk, r)
                                r += 1
                        while r < upto:
                            region(s + 1, nq, nk, r)
                            r += 1
                        if kt == KT - 2:
                            transpose_neg(s + 1)
                    sums(s, c, KT - 1)

                pairs_loop(pe, step)

        at[0] = 0
        xnt2 = take([P, 2 * KD, BANK])
        hidden = take([P, 2 * HT, BANK])
        w_down = take([P, HT, D])
        bias_up = take([P, 2, HT])

        ps_h = psum[:, 0:4, :]
        ps_d = psum[:, 4:8, :]

        s_bup = sem("up_bias_loaded")
        s_wt_ps = sem("w_down_transposed")
        s_wt = sem("w_down_copied")
        s_bias_ps = sem("bias_row_turned")
        s_bias = sem("bias_added")
        s_xnt2 = [sem(f"xn_transposed_loaded{n}") for n in range(2)]
        s_h_ps = sem("hidden_multiplied")
        s_h = sem("gelu_done")
        s_d_ps = sem("down_multiplied")
        s_d = sem("down_added")
        s_out = sem("out_stored")

        def ffn_loop(engine, step):
            with engine.Fori(0, CHUNKS // 2) as i:
                for p in range(2):
                    step(2 * i + p, i, p)

        with nc.Block() as block:
            @block.sync
            def _(sp):
                sp.dma_start(bias_up[:, 0, :], up_bias_columns).then_inc(s_bup, 16)

                def load(c, p):
                    sp.dma_start(xnt2[:, KD * p:KD * p + KD, :], xnt_dram[:, :, bass.ds(BANK * c, BANK)]).then_inc(s_xnt2[p], 16)

                load(0, 0)
                load(1, 1)

                def step(c, p, more=True):
                    if more:
                        sp.wait_ge(s_h_ps, HT * c + HT)
                        load(c + 2, p)
                    sp.wait_ge(s_d, c + 1)
                    tiles = bass.ds(CT * c, CT)
                    sp.dma_start(out_tiles[:, tiles, :], y[:, tiles, :]).then_inc(s_out, 16)

                with sp.Fori(0, CHUNKS // 2 - 1) as i:
                    for p in range(2):
                        step(2 * i + p, p)
                for p in range(2):
                    step(CHUNKS - 2 + p, p, more=False)
                sp.wait_ge(s_out, 16 * CHUNKS)
                for p in range(2):
                    sp.wait_ge(s_xnt2[p], 16 * CHUNKS // 2)

            @block.tensor
            def _(pe):
                for m in range(HT):
                    if m >= 4:
                        pe.wait_ge(s_wt, m - 3)
                    for k in range(KD):
                        last = nc.tensor.transpose(ps_h[:, m % 4, P * k:P * k + P],
                                                   w_down_t[:, k, P * m:P * m + P], ident[:, :])
                    last.then_inc(s_wt_ps, 1)
                for m in range(HT):
                    last = nc.tensor.matmul(ps_d[:, 0, m:m + 1], w_up[0:1, 2, P * m:P * m + P], one[0:1, 0:1],
                                            start=True, stop=True)
                last.then_inc(s_bias_ps, 1)
                pe.wait_ge(s_wt, HT)
                pe.wait_ge(s_bias, 1)

                def up(c, i, p):
                    pe.wait_ge(s_xnt2[p], 16 * (i + 1))
                    for m in range(HT):
                        pe.wait_ge(s_h, HT * c if m < 4 else HT * c + m - 3)
                        for k in range(KD):
                            last = nc.tensor.matmul(ps_h[:, m % 4, :], w_up[:, k, P * m:P * m + P],
                                                    xnt2[:, KD * p + k, :], start=(k == 0), stop=(k == KD - 1))
                        last.then_inc(s_h_ps, 1)

                def down(c, p):
                    pe.wait_ge(s_d, c)
                    for m in range(HT):
                        pe.wait_ge(s_h, HT * c + m + 1)
                        for t in range(CT):
                            last = nc.tensor.matmul(ps_d[:, t, 0:D], hidden[:, HT * p + m, P * t:P * t + P],
                                                    w_down[:, m, :], start=(m == 0), stop=(m == HT - 1))
                    last.then_inc(s_d_ps, 1)

                def step(c, i, p):
                    up(c, i, p)
                    down(c, p)

                ffn_loop(pe, step)

            @block.scalar
            def _(act):
                act.wait_ge(s_bias, 1)

                def step(c, i, p):
                    for m in range(HT):
                        act.wait_ge(s_h_ps, HT * c + m + 1)
                        nc.scalar.activation(hidden[:, HT * p + m, :], ps_h[:, m % 4, :], ACT.Gelu,
                                             bias=bias_up[:, 1, m:m + 1]).then_inc(s_h, 1)

                ffn_loop(act, step)

            @block.vector
            def _(dve):
                for m in range(HT):
                    dve.wait_ge(s_wt_ps, m + 1)
                    nc.vector.tensor_copy(w_down[:, m, :], ps_h[:, m % 4, 0:D]).then_inc(s_wt, 1)
                dve.wait_ge(s_bup, 16)
                dve.wait_ge(s_bias_ps, 1)
                nc.vector.tensor_tensor(bias_up[:, 1, :], bias_up[:, 0, :], ps_d[:, 0, 0:HT], ALU.add).then_inc(s_bias, 1)

                def step(c, i, p):
                    dve.wait_ge(s_d_ps, c + 1)
                    tiles = y[:, bass.ds(CT * c, CT), :]
                    nc.vector.tensor_tensor(tiles, ps_d[:, :, 0:D], tiles, ALU.add).then_inc(s_d, 1)

                ffn_loop(dve, step)


def kernel(L0_attn_x, L0_attn_W_qkv, L0_attn_b_qkv, L0_ffn_W_exp, L0_ffn_b_exp, L0_ffn_up_weights, L0_ffn_up_bias,
           L0_ffn_down_weights, L0_ffn_W_con, L0_ffn_b_con, L0_ffn_down_bias):
    import numpy as np
    import concourse.bacc as bacc
    from concourse.bass_utils import run_bass_kernel_spmd

    def planes(weights):
        return np.ascontiguousarray(np.asarray(weights).transpose(0, 2, 3, 1))

    def columns(vector):
        return np.asarray(vector).reshape(-1, P).T

    D = L0_attn_x.shape[-1]
    data = {
        "x": np.asarray(L0_attn_x), "w_qkv": np.asarray(L0_attn_W_qkv), "b_qk_columns": columns(L0_attn_b_qkv[:2 * D]),
        "b_v": np.asarray(L0_attn_b_qkv[2 * D:]),
        "w_exp": np.asarray(L0_ffn_W_exp), "b_exp": np.asarray(L0_ffn_b_exp),
        "up_planes": planes(L0_ffn_up_weights), "up_bias_columns": columns(L0_ffn_up_bias),
        "down_planes": planes(L0_ffn_down_weights),
        "w_con_t": np.ascontiguousarray(np.asarray(L0_ffn_W_con).transpose(1, 0)),
        "b_con": np.asarray(L0_ffn_b_con), "down_bias": np.asarray(L0_ffn_down_bias),
    }
    nc = bacc.Bacc("TRN2", target_bir_lowering=False, num_devices=1)
    arrays, args = {}, []
    for name, a in data.items():
        a = np.ascontiguousarray(a)
        arrays[f"in_{name}"] = a
        args.append(nc.dram_tensor(f"in_{name}", a.shape, mybir.dt.from_np(a.dtype), kind="ExternalInput").ap())
    shape = data["x"].shape
    out = nc.dram_tensor("out", shape, F32, kind="ExternalOutput").ap()
    attention_and_butterfly_ffn(nc, *args, out)
    result = run_bass_kernel_spmd(nc, [arrays], core_ids=[0])
    return result.results[0]["out"]
```

```python
from contextlib import ExitStack

import concourse.bass as bass
from concourse import mybir

F32 = mybir.dt.float32
BF16 = mybir.dt.bfloat16
ALU = mybir.AluOpType
ACT = mybir.ActivationFunctionType
AX_X = mybir.AxisListType.X

P = 128
BANK = 512
EPS = 1e-5
HEADS = 16


class Chain:

    def __init__(self, engine, sem, done=0):
        self.engine, self.sem, self.done = engine, sem, done

    def __call__(self, instruction):
        self.done = self.done + 1
        instruction.then_inc(self.sem, 1)
        self.engine.wait_ge(self.sem, self.done)


def attention_and_butterfly_ffn(nc, x, w_qkv, b_qk_columns, b_v, w_exp, b_exp, up_planes, up_bias_columns, down_planes,
                                w_con_t, b_con, down_bias, out):
    B, N, D = x.shape
    HD = D // HEADS
    KD = D // P
    TILES = B * N // P
    CT = BANK // P
    CHUNKS = TILES // CT
    HID = w_exp.shape[1]
    HT = HID // P
    STAGES = up_planes.shape[0]
    PAIRS = HID // 2
    QB = 2048
    SUPER = B * N * HEADS // QB
    QG = QB // BANK
    QT = QB // P
    KT = N // P
    PARTS = 3
    ROWS = 6 * HD
    VW = 32
    REGIONS = QT * N // (2 * BANK)
    PER_KT = REGIONS // KT
    MAX_PARTS = 2
    AHEAD = 16
    BEHIND = 8

    q_dram = nc.dram_tensor("q_parts", [PARTS, B * D, N], BF16, kind="Internal").ap()
    k_dram = nc.dram_tensor("k_parts", [PARTS, B * D, N], BF16, kind="Internal").ap()
    v_dram = nc.dram_tensor("v_columns", [B * HEADS, P, KT, HD], F32, kind="Internal").ap()
    xnt_dram = nc.dram_tensor("xn_transposed", [P, KD, B * N], F32, kind="Internal").ap()

    x_tiles = x.rearrange("b (t p) d -> p (b t) d", p=P)
    out_tiles = out.rearrange("b (t p) d -> p (b t) d", p=P)

    with ExitStack() as ctx:
        def sb(name, shape, dt=F32):
            return ctx.enter_context(nc.sbuf_tensor(name, shape, dt))

        def sem(name):
            return ctx.enter_context(nc.semaphore(name))

        psum = ctx.enter_context(nc.psum_tensor("psum", [P, 8, BANK], F32))
        y = sb("y", [P, TILES, D])
        ident = sb("ident", [P, P])
        ident_bf = sb("ident_bf", [P, P], BF16)
        one = sb("one", [1, 2])
        w_up = sb("w_up", [P, 3, HID])
        w_down_t = sb("w_down_t", [P, KD, HID])
        planes = sb("planes", [P, 2, 4, PAIRS])
        fold = sb("fold", [P, 3, 3, PAIRS])

        arena = sb("arena", [P, 18432])
        at = [0]

        def take(shape, dt=F32):
            words = 1
            for n in shape[1:]:
                words *= n
            if dt == BF16:
                words //= 2
            ap = arena[0:shape[0], at[0]:at[0] + words]
            at[0] += words
            assert at[0] <= 18432
            if dt == BF16:
                ap = ap.bitcast(BF16)
            if len(shape) == 3:
                ap = ap.rearrange("p (a b) -> p a b", b=shape[2])
            if len(shape) == 4:
                ap = ap.rearrange("p (a b c) -> p a b c", b=shape[2], c=shape[3])
            return ap

        def row(vector, n=P):
            return vector.rearrange("(a d) -> a d", a=1).to_broadcast([n, vector.shape[0]])

        wqkv = take([P, KD, 3 * D])
        bqk = take([P, 2 * KD])
        bv = take([P, D])
        btail = take([P, 2, D])
        stats = take([P, 2 * CT, 6])
        mv = take([P, 2 * CT, 2])
        std = take([P, 2, CT])
        rstd = take([P, 2, CT])
        eps = take([P, 1])
        wait_slot = take([P, 1])
        xn = take([P, 2 * CT, D])
        xnt = take([P, 2 * KD, BANK])
        full = take([P, 2 * KD, BANK])
        rest = take([P, 2, BANK])
        v_sb = take([P, 2 * HEADS, CT * HD])
        parts = take([P, 2 * KD * PARTS, BANK], BF16)

        ps_xt, ps_qk, ps_v = psum[:, 0:2, :], psum[:, 2:6, :], psum[:, 6:8, :]

        s_w = sem("weights_loaded")
        s_ident = sem("ident_made")
        s_x = [sem(f"x_loaded{n}") for n in range(2)]
        s_moments = sem("moments_done")
        s_std = sem("std_done")
        s_rstd = sem("rstd_done")
        s_xn = sem("xn_done")
        s_res = sem("residual_bias_added")
        s_xt_ps = sem("xt_transposed")
        s_xt = sem("xt_copied")
        s_qk_ps = sem("qk_multiplied")
        s_full = sem("qk_full_copied")
        s_high = sem("high_part_done")
        s_parts = sem("parts_done")
        s_v_ps = sem("v_multiplied")
        s_v = sem("v_done")
        s_dve = sem("dve_chain1")
        s_parts_out = [sem(f"parts_stored{n}") for n in range(2 * KD)]
        s_v_out = [sem(f"v_stored{n}") for n in range(2)]
        s_xt_out = [sem(f"xt_stored{n}") for n in range(2)]

        def chunk_loop(engine, step, head=0):
            with engine.Fori(0, CHUNKS // 2 - 2) as i:
                for p in range(2):
                    step(2 * i + p, i, p, CHUNKS)
            for c in range(CHUNKS - 4, CHUNKS):
                step(c, c // 2, c % 2, CHUNKS - c)

        with nc.Block() as block:
            @block.gpsimd
            def _(pool):
                nc.gpsimd.memset(ident[:, :], 0.0).then_inc(s_ident, 1)
                nc.gpsimd.memset(ident_bf[:, :], 0.0).then_inc(s_ident, 1)
                nc.gpsimd.memset(one[:, :], 1.0).then_inc(s_ident, 1)
                nc.gpsimd.memset(eps, EPS).then_inc(s_ident, 1)
                pool.wait_ge(s_ident, 4)
                for m in (ident, ident_bf):
                    nc.gpsimd.affine_select(out=m[:, :], in_=m[:, :], compare_op=ALU.not_equal, fill=1.0,
                                            base=0, pattern=[[-1, P]], channel_multiplier=1).then_inc(s_ident, 1)
                pool.wait_ge(s_w, 16 * 5)
                nc.gpsimd.tensor_tensor(btail[:, 0, :], btail[:, 0, :], btail[:, 1, :], ALU.add).then_inc(s_res, 1)
                pool.wait_ge(s_res, 1)
                tail_bias = btail[:, 0, :].unsqueeze(1).to_broadcast([P, CT, D])
                with pool.Fori(0, CHUNKS) as c:
                    pool.wait_ge(s_xn, CT * c + CT)
                    tiles = y[:, bass.ds(CT * c, CT), :]
                    nc.gpsimd.tensor_tensor(tiles, tiles, tail_bias, ALU.add).then_inc(s_res, 1)

            @block.sync
            def _(sp):
                sp.dma_start(y[:, 0:CT, :], x_tiles[:, 0:CT, :]).then_inc(s_x[0], 16)
                sp.dma_start(y[:, CT:2 * CT, :], x_tiles[:, CT:2 * CT, :]).then_inc(s_x[1], 16)
                sp.dma_start(wqkv, w_qkv.rearrange("(k p) n -> p k n", p=P)).then_inc(s_w, 16)
                sp.dma_start(bqk, b_qk_columns).then_inc(s_w, 16)
                sp.dma_start(bv, row(b_v)).then_inc(s_w, 16)
                sp.dma_start(btail[:, 0, :], row(b_con)).then_inc(s_w, 16)
                sp.dma_start(btail[:, 1, :], row(down_bias)).then_inc(s_w, 16)
                for c in range(2, 4):
                    sp.wait_ge(s_moments, 2 * CT * (c - 1))
                    sp.dma_start(y[:, CT * c:CT * c + CT, :], x_tiles[:, CT * c:CT * c + CT, :]).then_inc(s_x[c % 2], 16)

                def step(c, i, p, left):
                    if left > 4:
                        sp.wait_ge(s_moments, 2 * CT * (c + 3))
                        sp.dma_start(y[:, bass.ds(CT * c + 4 * CT, CT), :],
                                     x_tiles[:, bass.ds(CT * c + 4 * CT, CT), :]).then_inc(s_x[p], 16)
                    b, of_row = c // (CHUNKS // B), c % (CHUNKS // B)
                    sp.wait_ge(s_xt, KD * c + KD)
                    sp.dma_start(xnt_dram[:, :, bass.ds(BANK * c, BANK)], xnt[:, KD * p:KD * p + KD, :]).then_inc(s_xt_out[p], 16)
                    for m in range(2 * KD):
                        sp.wait_ge(s_parts, 2 * KD * c + m + 1)
                        rows = bass.ds(D * b + P * (m % KD), P)
                        dst = (q_dram if m < KD else k_dram)[:, rows, bass.ds(BANK * of_row, BANK)]
                        sp.dma_start(dst.rearrange("n r k -> r n k"), parts[:, PARTS * m:PARTS * m + PARTS, :])\
                          .then_inc(s_parts_out[m], 16)
                    sp.wait_ge(s_v, 2 * c + 2)
                    dst = v_dram[bass.ds(HEADS * b, HEADS), :, bass.ds(CT * of_row, CT), :].rearrange("h p t d -> p h (t d)")
                    sp.dma_start(dst, v_sb[:, HEADS * p:HEADS * p + HEADS, :]).then_inc(s_v_out[p], 16)

                chunk_loop(sp, step)
                for m in range(2 * KD):
                    sp.wait_ge(s_parts_out[m], 16 * CHUNKS)
                for p in range(2):
                    sp.wait_ge(s_v_out[p], 16 * CHUNKS // 2)
                    sp.wait_ge(s_xt_out[p], 16 * CHUNKS // 2)

            @block.scalar
            def _(act):
                def deviation(c, p):
                    act.wait_ge(s_moments, 2 * CT * c + 2 * CT)
                    nc.scalar.activation(std[:, p, :], mv[:, CT * p:CT * p + CT, 1], ACT.Sqrt, bias=eps).then_inc(s_std, 1)

                act.wait_ge(s_ident, 6)
                deviation(0, 0)
                deviation(1, 1)
                act.wait_ge(s_xt_ps, 1)
                for k in range(KD):
                    nc.scalar.copy(xnt[:, k, :], ps_xt[:, k, :]).then_inc(s_xt, 1)
                act.wait_ge(s_w, 16 * 5)

                def step(c, i, p, left):
                    if left > 1:
                        q = 1 - p
                        act.wait_ge(s_xt_ps, c + 2)
                        act.wait_ge(s_xt_out[q], 16 * (i + p))
                        act.wait_ge(s_v_ps, 2 * c)
                        for k in range(KD):
                            nc.scalar.copy(xnt[:, KD * q + k, :], ps_xt[:, k, :]).then_inc(s_xt, 1)
                    for m in range(2 * KD):
                        act.wait_ge(s_qk_ps, 2 * KD * c + m + 1)
                        act.wait_ge(s_parts, 2 * KD * c)
                        dst, src = full[:, m, :], ps_qk[:, m, :]
                        if m < KD:
                            dst = dst.rearrange("p (t k) -> p k t", t=QT)
                            src = src.rearrange("p (k t) -> p k t", t=QT)
                        nc.scalar.activation(dst, src, ACT.Identity, bias=bqk[:, m:m + 1]).then_inc(s_full, 1)
                        act.wait_ge(s_full, 2 * KD * c + m + 1)
                        act.wait_ge(s_parts_out[m], 16 * c)
                        nc.scalar.copy(parts[:, PARTS * m, :], full[:, m, :]).then_inc(s_high, 1)
                    if left > 2:
                        deviation(c + 2, p)

                chunk_loop(act, step)

            @block.vector
            def _(dve):
                def x_tile(c, t):
                    return y[:, bass.ds(CT * c + t, 1), :].rearrange("p o d -> p (o d)")

                def moments(c, i, p, again=True):
                    dve.wait_ge(s_x[p], 16 * i + 16)
                    if again:
                        dve.wait_ge(s_xn, CT * c - CT)
                    for t in range(CT):
                        nc.vector.bn_stats(stats[:, CT * p + t, :], x_tile(c, t)).then_inc(s_moments, 1)
                    dve.wait_ge(s_moments, 2 * CT * c + CT)
                    nc.vector.memset(wait_slot, 0.0)
                    for t in range(CT):
                        nc.vector.bn_aggr(mv[:, CT * p + t, :], stats[:, CT * p + t, :]).then_inc(s_moments, 1)

                def normalise(c, p, again=True):
                    dve.wait_ge(s_std, c + 1)
                    if again:
                        dve.wait_ge(s_xt_ps, c - 1)
                    nc.vector.reciprocal(rstd[:, p, :], std[:, p, :]).then_inc(s_rstd, 1)
                    dve.wait_ge(s_rstd, c + 1)
                    for t in range(CT):
                        nc.vector.tensor_scalar(xn[:, CT * p + t, :], x_tile(c, t), mv[:, CT * p + t, 0:1],
                                                rstd[:, p, t:t + 1], ALU.subtract, ALU.mult).then_inc(s_xn, 1)

                for c in range(2):
                    moments(c, 0, c, again=False)
                    normalise(c, c, again=False)
                dve.wait_ge(s_w, 16 * 5)
                bv_pair = bv.unsqueeze(1).to_broadcast([P, 2, D]).rearrange("p t (h d) -> p t h d", d=HD)

                def split(c, m):
                    dve.wait_ge(s_high, 2 * KD * c + m + 1)
                    chain = Chain(dve, s_dve, 2 * (2 * KD * c + m))
                    r = rest[:, m % 2, :]
                    chain(nc.vector.tensor_tensor(r, full[:, m, :], parts[:, PARTS * m, :], ALU.subtract))
                    chain(nc.vector.tensor_copy(parts[:, PARTS * m + 1, :], r))
                    nc.vector.tensor_tensor(parts[:, PARTS * m + 2, :], r, parts[:, PARTS * m + 1, :], ALU.subtract)\
                      .then_inc(s_parts, 1)

                def step(c, i, p, left):
                    if left > 2:
                        moments(c + 2, i + 1, p)
                    for m in range(2):
                        split(c, m)
                    if left > 2:
                        normalise(c + 2, p)
                    for m in range(2, 2 * KD):
                        split(c, m)
                    dve.wait_ge(s_v_out[p], 16 * i)
                    for t in range(2):
                        dve.wait_ge(s_v_ps, 2 * c + t + 1)
                        dst = v_sb[:, HEADS * p:HEADS * p + HEADS, 2 * HD * t:2 * HD * t + 2 * HD]
                        nc.vector.tensor_tensor(dst.rearrange("p h (t d) -> p t h d", d=HD),
                                                ps_v[:, t, :].rearrange("p (t h d) -> p t h d", t=2, d=HD), bv_pair, ALU.add)\
                          .then_inc(s_v, 1)

                chunk_loop(dve, step)

            @block.tensor
            def _(pe):
                def transposes(c, p):
                    pe.wait_ge(s_xn, CT * c + CT)
                    pe.wait_ge(s_xt, KD * c)
                    for k in range(KD):
                        for t in range(CT):
                            last = nc.tensor.transpose(ps_xt[:, k, P * t:P * t + P],
                                                       xn[:, CT * p + t, P * k:P * k + P], ident[:, :])
                    last.then_inc(s_xt_ps, 1)

                pe.wait_ge(s_ident, 6)
                transposes(0, 0)
                pe.wait_ge(s_w, 16 * 5)

                def step(c, i, p, left):
                    if left > 1:
                        transposes(c + 1, 1 - p)
                    pe.wait_ge(s_xt, KD * c + KD)
                    pe.wait_ge(s_full, 2 * KD * c)
                    for m in range(2 * KD):
                        for k in range(KD):
                            last = nc.tensor.matmul(ps_qk[:, m, :], wqkv[:, k, P * m:P * m + P],
                                                    xnt[:, KD * p + k, :], start=(k == 0), stop=(k == KD - 1))
                        last.then_inc(s_qk_ps, 1)
                    pe.wait_ge(s_v, 2 * c)
                    for t in range(CT):
                        for k in range(KD):
                            last = nc.tensor.matmul(ps_v[:, t // 2, (t % 2) * D:(t % 2) * D + D],
                                                    xnt[:, KD * p + k, P * t:P * t + P],
                                                    wqkv[:, k, 2 * D:3 * D], start=(k == 0), stop=(k == KD - 1))
                        if t % 2:
                            last.then_inc(s_v_ps, 1)

                chunk_loop(pe, step)

        at[0] = 0
        k_rows = take([P, 2, N], BF16)
        q_rows = take([P, 4, QB], BF16)
        probs = take([P, 4, QG * BANK])
        v_cols = take([P, 2 * KT, VW])
        o_t = sb("o_t", [P, QT, VW])
        maxima = sb("maxima", [P, 2, REGIONS])
        neg_max = sb("neg_max", [P, QT])
        neg_parts = sb("neg_parts", [P, MAX_PARTS * QT], BF16)
        neg_rows = sb("neg_rows", [MAX_PARTS * QT, P], BF16)
        recip = sb("recip", [P, QT])

        ps_max = [psum[:, 0:2, :], psum[:, 2:4, :]]
        ps_s = psum[:, 4:6, :]
        ps_o = psum[:, 6:8, :]
        ps_neg = [psum[0:MAX_PARTS * QT, 6 + n, 0:P // 2].bitcast(BF16) for n in range(2)]

        s_q = [sem(f"q_rows_loaded{n}") for n in range(4)]
        s_k = [sem(f"k_rows_loaded{n}") for n in range(2)]
        s_vc = [sem(f"v_cols_loaded{n}") for n in range(2)]
        s_set = sem("constants_set")
        s_region = sem("region_multiplied")
        s_region_free = sem("region_slot_free")
        s_fin = sem("maxima_finished")
        s_rows = sem("neg_rows_transposed")
        s_rows_sb = sem("neg_rows_copied")
        s_neg_in = sem("neg_rows_in_place")
        s_score = sem("scores_multiplied")
        s_exp = sem("exps_done")
        s_pv = sem("probs_used")
        s_o_free = sem("o_banks_free")
        s_evac = sem("sums_taken")
        s_plane = [sem(f"planes_loaded{n}") for n in range(2)]
        s_wld = sem("ffn_weights_loaded")
        s_fold = sem("pool_chain")
        LOADS = 3
        ROWS_KT = (REGIONS - AHEAD) // PER_KT + 3
        FIN = 3
        EVAC = 3

        def superblocks(engine, step):
            with engine.Fori(0, SUPER // 4 - 1) as i:
                for c in range(4):
                    step(4 * i + c, c, i, False)
            i = SUPER // 4 - 1
            for c in range(4):
                step(4 * i + c, c, i, True)

        with nc.Block() as block:
            @block.gpsimd
            def _(pool):
                ones = Chain(pool, s_set)
                ones(nc.gpsimd.memset(k_rows[ROWS:ROWS + MAX_PARTS, :, :], 1.0))
                ones(nc.gpsimd.memset(v_cols[:, :, HD:HD + 1], 1.0))
                ones(nc.gpsimd.memset(v_cols[:, :, HD + 1:VW], 0.0))
                chain = Chain(pool, s_fold)
                chain(nc.gpsimd.memset(w_up[:, 2, :], 0.0))
                pool.dma_start(w_up[:, 0:KD, :], w_exp.rearrange("(k p) n -> p k n", p=P)).then_inc(s_wld, 16)
                pool.dma_start(w_up[0:1, 2, :], row(b_exp, 1)).then_inc(s_wld, 16)
                pool.dma_start(w_down_t[:, :, :], w_con_t.rearrange("(k p) n -> p k n", p=P)).then_inc(s_wld, 16)
                pool.wait_ge(s_wld, 48)
                turns = [(w_up, 3, up_planes, s) for s in range(STAGES)]
                turns += [(w_down_t, KD, down_planes, s) for s in reversed(range(STAGES))]

                def load_planes(n):
                    _, _, src, s = turns[n]
                    flat = src[s].rearrange("a b k -> (a b k)")
                    pool.dma_start(planes[:, n % 2, :, :].rearrange("p a k -> p (a k)"), row(flat)).then_inc(s_plane[n % 2], 16)

                load_planes(0)
                for n, (w, rows, _, s) in enumerate(turns):
                    if n + 1 < len(turns):
                        load_planes(n + 1)
                    pool.wait_ge(s_plane[n % 2], 16 * (n // 2 + 1))
                    stride = 2 ** s
                    pair = w[:, :, :].rearrange("p r (n two s) -> p r n two s", two=2, s=stride)
                    down = w is w_down_t
                    for r in range(rows):
                        a, b = pair[:, r, :, 0, :], pair[:, r, :, 1, :]

                        def plane(to, of):
                            index = 2 * of + to if down else 2 * to + of
                            return planes[:, n % 2, index, :].rearrange("p (n s) -> p n s", s=stride)

                        def tmp(q):
                            return fold[:, r, q, :].rearrange("p (n s) -> p n s", s=stride)

                        mult, add = ALU.mult, ALU.add
                        nc.gpsimd.tensor_tensor(tmp(0), a, plane(0, 0), mult).then_inc(s_fold, 1)
                        nc.gpsimd.tensor_tensor(tmp(1), b, plane(0, 1), mult).then_inc(s_fold, 1)
                        chain.done += 2
                        chain(nc.gpsimd.tensor_tensor(tmp(2), a, plane(1, 0), mult))
                        chain(nc.gpsimd.tensor_tensor(a, tmp(0), tmp(1), add))
                        chain(nc.gpsimd.tensor_tensor(tmp(0), b, plane(1, 1), mult))
                        chain(nc.gpsimd.tensor_tensor(b, tmp(2), tmp(0), add))

            @block.sync
            def _(sp):
                def load_q(head, half, slot):
                    for first, part, copies in ((0, 0, 3), (3, 1, 2), (5, 2, 1)):
                        src = q_dram[part:part + 1, bass.ds(HD * head, HD), QB * half:QB * half + QB].to_broadcast([copies, HD, QB])
                        sp.dma_start(q_rows[HD * first:HD * (first + copies), slot, :], src).then_inc(s_q[slot], 16)

                def load_k(head, slot):
                    for first, count in ((0, 3), (3, 2), (5, 1)):
                        src = k_dram[0:count, bass.ds(HD * head, HD), :]
                        sp.dma_start(k_rows[HD * first:HD * (first + count), slot, :], src).then_inc(s_k[slot], 16)

                def load_v(n, slot):
                    src = v_dram[bass.ds(n, 1), :, :, :].rearrange("o p t d -> (o p) t d")
                    sp.dma_start(v_cols[:, KT * slot:KT * slot + KT, 0:HD], src).then_inc(s_vc[slot], 16)

                def place_neg(n, slot):
                    sp.wait_ge(s_rows_sb, n + 1)
                    sp.dma_start(q_rows[ROWS:ROWS + MAX_PARTS, slot, :], neg_rows[:, :]).then_inc(s_neg_in, 16)

                load_k(0, 0)
                load_q(0, 0, 0)
                load_v(0, 0)
                load_q(0, 1, 1)
                place_neg(0, 0)

                def step(s, c, i, last):
                    head = 2 * i + c // 2 + 1
                    more = not (last and c >= 2)
                    sp.wait_ge(s_score, KT * QG * s)
                    if more:
                        load_q(head, c % 2, (c + 2) % 4)
                    if more and c % 2 == 0:
                        load_k(head, (c // 2 + 1) % 2)
                        sp.wait_ge(s_pv, KT * s + 4)
                        load_v(head, (c // 2 + 1) % 2)
                    if not (last and c == 3):
                        place_neg(s + 1, (c + 1) % 4)

                superblocks(sp, step)
                sp.wait_ge(s_neg_in, 16 * SUPER)
                for n in range(4):
                    sp.wait_ge(s_q[n], 16 * LOADS * SUPER // 4)
                for n in range(2):
                    sp.wait_ge(s_k[n], 16 * LOADS * SUPER // 4)
                    sp.wait_ge(s_vc[n], 16 * SUPER // 4)

            @block.scalar
            def _(act):
                def step(s, c, i, last):
                    for kt in range(KT):
                        act.wait_ge(s_pv, KT * s + kt + 1)
                        for g in range(QG):
                            act.wait_ge(s_score, QG * (KT * s + kt) + g + 1)
                            nc.scalar.activation(probs[:, kt % 4, BANK * g:BANK * g + BANK], ps_s[:, g % 2, :],
                                                 ACT.Exp).then_inc(s_exp, 1)

                superblocks(act, step)

            @block.vector
            def _(dve):
                for n, (signal, count) in enumerate(((s_region_free, 2), (s_exp, 2), (s_pv, 4), (s_o_free, 2))):
                    nc.vector.memset(recip[:, n:n + 1], 0.0).then_inc(signal, count)

                def reduce_region(m, n, parity):
                    dve.wait_ge(s_region, REGIONS * m + n + 1)
                    nc.vector.tensor_reduce(maxima[:, parity, n:n + 1], ps_max[n % 2].rearrange("p a b -> p (a b)"),
                                            axis=AX_X, op=ALU.max).then_inc(s_region_free, 1)

                def finish_maxima(m, parity):
                    high, low = neg_parts[:, 0:QT], neg_parts[:, QT:2 * QT]

                    def negate():
                        dve.wait_ge(s_region_free, REGIONS * m + REGIONS + 2)
                        nc.vector.tensor_reduce(neg_max[:, :], maxima[:, parity, :].rearrange("p (t r) -> p t r", t=QT),
                                                axis=AX_X, op=ALU.max, negate=True).then_inc(s_fin, 1)

                    def high_part():
                        dve.wait_ge(s_fin, FIN * m + 1)
                        nc.vector.tensor_copy(high, neg_max[:, :]).then_inc(s_fin, 1)

                    def low_part():
                        dve.wait_ge(s_fin, FIN * m + 2)
                        nc.vector.tensor_tensor(low, neg_max[:, :], high, ALU.subtract).then_inc(s_fin, 1)

                    def copy_rows():
                        dve.wait_ge(s_neg_in, 16 * m)
                        dve.wait_ge(s_rows, m + 1)
                        nc.vector.tensor_copy(neg_rows[:, :], ps_neg[parity]).then_inc(s_rows_sb, 1)

                    return [negate, high_part, low_part, copy_rows]

                def take_sums(s, c):
                    dims = o_t[:, :, 0:HD]
                    dst = y[:, bass.ds(s, 1), :].rearrange("p o (t d) -> p (o t) d", d=HD)

                    def turn():
                        dve.wait_ge(s_pv, KT * s + KT + 4)
                        dve.wait_ge(s_evac, EVAC * s)
                        nc.vector.transpose(o_t[:, :, :].rearrange("p t v -> p (t v)"), ps_o[:, c % 2, :]).then_inc(s_o_free, 1)

                    def invert():
                        dve.wait_ge(s_o_free, s + 3)
                        nc.vector.reciprocal(recip[:, :], o_t[:, :, HD]).then_inc(s_evac, 1)

                    def scale():
                        dve.wait_ge(s_evac, EVAC * s + 1)
                        nc.vector.tensor_tensor(dims, dims, recip[:, :].unsqueeze(2).to_broadcast([P, QT, HD]), ALU.mult)\
                          .then_inc(s_evac, 1)

                    def add():
                        dve.wait_ge(s_evac, EVAC * s + 2)
                        nc.vector.tensor_tensor(dst, dst, dims, ALU.add).then_inc(s_evac, 1)

                    return [turn, invert, scale, add]

                for n in range(REGIONS):
                    reduce_region(0, n, 0)
                for f in finish_maxima(0, 0):
                    f()
                for n in range(AHEAD + BEHIND):
                    reduce_region(1, n, 1)

                def step(s, c, i, last):
                    after = {}
                    for q, f in enumerate(finish_maxima(s + 1, (c + 1) % 2)):
                        after[REGIONS - AHEAD - BEHIND - 1 + PER_KT * (q if q < 3 else 4)] = f
                    for q, f in enumerate(take_sums(s, c)):
                        after[REGIONS - BEHIND + PER_KT * q + PER_KT - 1] = f
                    for r in range(REGIONS):
                        m, n = divmod(AHEAD + BEHIND + r, REGIONS)
                        m += c + 1 - 4 * (last is True)
                        if not last or m < 0:
                            reduce_region(m + (4 * i if not last else SUPER), n, m % 2)
                        if r in after and not (last and c == 3 and r < REGIONS - BEHIND):
                            after[r]()

                superblocks(dve, step)

            @block.tensor
            def _(pe):
                def region_half(m, c, n, half):
                    if half == 0:
                        pe.wait_ge(s_region_free, REGIONS * m + n + 1)
                    t, keys = n // 4, (n % 4 * 2 + half) * BANK
                    mm = nc.tensor.matmul(ps_max[n % 2][:, half, :], q_rows[0:ROWS, c, P * t:P * t + P],
                                          k_rows[0:ROWS, c // 2, keys:keys + BANK], start=True, stop=True)
                    if half == 1:
                        mm.then_inc(s_region, 1)

                def neg_to_rows(m, parity):
                    pe.wait_ge(s_fin, FIN * (m + 1))
                    pe.wait_ge(s_o_free, m + 1)
                    nc.tensor.transpose(ps_neg[parity], neg_parts[:, :], ident_bf[:, :]).then_inc(s_rows, 1)

                def scores(s, c, kt, g):
                    if kt == 0 and g == 0:
                        pe.wait_ge(s_neg_in, 16 * (s + 1))
                    pe.wait_ge(s_exp, QG * (KT * s + kt) + g + 1)
                    nc.tensor.matmul(ps_s[:, g % 2, :], k_rows[0:ROWS + MAX_PARTS, c // 2, P * kt:P * kt + P],
                                     q_rows[0:ROWS + MAX_PARTS, c, BANK * g:BANK * g + BANK],
                                     start=True, stop=True).then_inc(s_score, 1)

                def sums(s, c, kt):
                    if kt == 0:
                        pe.wait_ge(s_o_free, s + 1)
                    pe.wait_ge(s_exp, QG * (KT * s + kt + 1) + 2)
                    for g in range(QG):
                        last = nc.tensor.matmul(ps_o[VW * g:VW * g + VW, c % 2, :], v_cols[:, KT * (c // 2) + kt, :],
                                                probs[:, kt % 4, BANK * g:BANK * g + BANK],
                                                start=(kt == 0), stop=(kt == KT - 1))
                    last.then_inc(s_pv, 1)

                pe.wait_ge(s_set, 3)
                pe.wait_ge(s_k[0], 16 * LOADS)
                pe.wait_ge(s_q[0], 16 * LOADS)
                for n in range(REGIONS):
                    region_half(0, 0, n, 0)
                    region_half(0, 0, n, 1)
                neg_to_rows(0, 0)
                pe.wait_ge(s_q[1], 16 * LOADS)
                for n in range(AHEAD):
                    region_half(1, 1, n, 0)
                    region_half(1, 1, n, 1)
                scores(0, 0, 0, 0)
                scores(0, 0, 0, 1)

                def step(s, c, i, last):
                    if c % 2 == 0:
                        pe.wait_ge(s_vc[c // 2], 16 * (i + 1))
                    for kt in range(KT):
                        halves = []
                        for n in range(PER_KT):
                            d, n = divmod(AHEAD + PER_KT * kt + n, REGIONS)
                            to = c + 1 + d
                            if last and to >= 4:
                                continue
                            if d == 1 and n == 0:
                                pe.wait_ge(s_q[to % 4], 16 * LOADS * (i + 1 + to // 4))
                                pe.wait_ge(s_k[to // 2 % 2], 16 * LOADS * (i + 1 + to // 4))
                            halves += [(4 * i + to, to % 4, n, h) for h in range(2)]
                        if kt == ROWS_KT and not (last and c == 3):
                            neg_to_rows(s + 1, (c + 1) % 2)
                        scores(s, c, kt, 2)
                        for h in halves[0:1]:
                            region_half(*h)
                        scores(s, c, kt, 3)
                        for h in halves[1:3]:
                            region_half(*h)
                        if kt < KT - 1:
                            scores(s, c, kt + 1, 0)
                        elif not (last and c == 3):
                            scores(s + 1, (c + 1) % 4, 0, 0)
                        for h in halves[3:4]:
                            region_half(*h)
                        if kt < KT - 1:
                            scores(s, c, kt + 1, 1)
                        elif not (last and c == 3):
                            scores(s + 1, (c + 1) % 4, 0, 1)
                        sums(s, c, kt)

                superblocks(pe, step)

        at[0] = 0
        xnt2 = take([P, 2 * KD, BANK])
        hidden = take([P, 2 * HT, BANK])
        w_down = take([P, HT, D])
        bias_up = take([P, 2, HT])

        ps_h = psum[:, 0:4, :]
        ps_d = psum[:, 4:8, :]

        s_bup = sem("up_bias_loaded")
        s_wt_ps = sem("w_down_transposed")
        s_wt = sem("w_down_copied")
        s_bias_ps = sem("bias_row_turned")
        s_bias = sem("bias_added")
        s_xnt2 = [sem(f"xn_transposed_loaded{n}") for n in range(2)]
        s_h_ps = sem("hidden_multiplied")
        s_h = sem("gelu_done")
        s_d_ps = sem("down_multiplied")
        s_d = sem("down_added")
        s_out = sem("out_stored")

        def ffn_loop(engine, step):
            with engine.Fori(0, CHUNKS // 2) as i:
                for p in range(2):
                    step(2 * i + p, i, p)

        with nc.Block() as block:
            @block.sync
            def _(sp):
                sp.dma_start(bias_up[:, 0, :], up_bias_columns).then_inc(s_bup, 16)

                def load(c, p):
                    sp.dma_start(xnt2[:, KD * p:KD * p + KD, :], xnt_dram[:, :, bass.ds(BANK * c, BANK)]).then_inc(s_xnt2[p], 16)

                load(0, 0)
                load(1, 1)

                def step(c, p, more=True):
                    if more:
                        sp.wait_ge(s_h_ps, HT * c + HT)
                        load(c + 2, p)
                    sp.wait_ge(s_d, c + 1)
                    tiles = bass.ds(CT * c, CT)
                    sp.dma_start(out_tiles[:, tiles, :], y[:, tiles, :]).then_inc(s_out, 16)

                with sp.Fori(0, CHUNKS // 2 - 1) as i:
                    for p in range(2):
                        step(2 * i + p, p)
                for p in range(2):
                    step(CHUNKS - 2 + p, p, more=False)
                sp.wait_ge(s_out, 16 * CHUNKS)
                for p in range(2):
                    sp.wait_ge(s_xnt2[p], 16 * CHUNKS // 2)

            @block.tensor
            def _(pe):
                for m in range(HT):
                    if m >= 4:
                        pe.wait_ge(s_wt, m - 3)
                    for k in range(KD):
                        last = nc.tensor.transpose(ps_h[:, m % 4, P * k:P * k + P],
                                                   w_down_t[:, k, P * m:P * m + P], ident[:, :])
                    last.then_inc(s_wt_ps, 1)
                for m in range(HT):
                    last = nc.tensor.matmul(ps_d[:, 0, m:m + 1], w_up[0:1, 2, P * m:P * m + P], one[0:1, 0:1],
                                            start=True, stop=True)
                last.then_inc(s_bias_ps, 1)
                pe.wait_ge(s_wt, HT)
                pe.wait_ge(s_bias, 1)

                def up(c, i, p):
                    pe.wait_ge(s_xnt2[p], 16 * (i + 1))
                    for m in range(HT):
                        pe.wait_ge(s_h, HT * c if m < 4 else HT * c + m - 3)
                        for k in range(KD):
                            last = nc.tensor.matmul(ps_h[:, m % 4, :], w_up[:, k, P * m:P * m + P],
                                                    xnt2[:, KD * p + k, :], start=(k == 0), stop=(k == KD - 1))
                        last.then_inc(s_h_ps, 1)

                def down(c, p):
                    pe.wait_ge(s_d, c)
                    for m in range(HT):
                        pe.wait_ge(s_h, HT * c + m + 1)
                        for t in range(CT):
                            last = nc.tensor.matmul(ps_d[:, t, 0:D], hidden[:, HT * p + m, P * t:P * t + P],
                                                    w_down[:, m, :], start=(m == 0), stop=(m == HT - 1))
                    last.then_inc(s_d_ps, 1)

                def step(c, i, p):
                    up(c, i, p)
                    down(c, p)

                ffn_loop(pe, step)

            @block.scalar
            def _(act):
                act.wait_ge(s_bias, 1)

                def step(c, i, p):
                    for m in range(HT):
                        act.wait_ge(s_h_ps, HT * c + m + 1)
                        nc.scalar.activation(hidden[:, HT * p + m, :], ps_h[:, m % 4, :], ACT.Gelu,
                                             bias=bias_up[:, 1, m:m + 1]).then_inc(s_h, 1)

                ffn_loop(act, step)

            @block.vector
            def _(dve):
                for m in range(HT):
                    dve.wait_ge(s_wt_ps, m + 1)
                    nc.vector.tensor_copy(w_down[:, m, :], ps_h[:, m % 4, 0:D]).then_inc(s_wt, 1)
                dve.wait_ge(s_bup, 16)
                dve.wait_ge(s_bias_ps, 1)
                nc.vector.tensor_tensor(bias_up[:, 1, :], bias_up[:, 0, :], ps_d[:, 0, 0:HT], ALU.add).then_inc(s_bias, 1)

                def step(c, i, p):
                    dve.wait_ge(s_d_ps, c + 1)
                    tiles = y[:, bass.ds(CT * c, CT), :]
                    nc.vector.tensor_tensor(tiles, ps_d[:, :, 0:D], tiles, ALU.add).then_inc(s_d, 1)

                ffn_loop(dve, step)


def kernel(L0_attn_x, L0_attn_W_qkv, L0_attn_b_qkv, L0_ffn_W_exp, L0_ffn_b_exp, L0_ffn_up_weights, L0_ffn_up_bias,
           L0_ffn_down_weights, L0_ffn_W_con, L0_ffn_b_con, L0_ffn_down_bias):
    import numpy as np
    import concourse.bacc as bacc
    from concourse.bass_utils import run_bass_kernel_spmd

    def planes(weights):
        return np.ascontiguousarray(np.asarray(weights).transpose(0, 2, 3, 1))

    def columns(vector):
        return np.asarray(vector).reshape(-1, P).T

    D = L0_attn_x.shape[-1]
    data = {
        "x": np.asarray(L0_attn_x), "w_qkv": np.asarray(L0_attn_W_qkv), "b_qk_columns": columns(L0_attn_b_qkv[:2 * D]),
        "b_v": np.asarray(L0_attn_b_qkv[2 * D:]),
        "w_exp": np.asarray(L0_ffn_W_exp), "b_exp": np.asarray(L0_ffn_b_exp),
        "up_planes": planes(L0_ffn_up_weights), "up_bias_columns": columns(L0_ffn_up_bias),
        "down_planes": planes(L0_ffn_down_weights),
        "w_con_t": np.ascontiguousarray(np.asarray(L0_ffn_W_con).transpose(1, 0)),
        "b_con": np.asarray(L0_ffn_b_con), "down_bias": np.asarray(L0_ffn_down_bias),
    }
    nc = bacc.Bacc("TRN2", target_bir_lowering=False, num_devices=1)
    arrays, args = {}, []
    for name, a in data.items():
        a = np.ascontiguousarray(a)
        arrays[f"in_{name}"] = a
        args.append(nc.dram_tensor(f"in_{name}", a.shape, mybir.dt.from_np(a.dtype), kind="ExternalInput").ap())
    shape = data["x"].shape
    out = nc.dram_tensor("out", shape, F32, kind="ExternalOutput").ap()
    attention_and_butterfly_ffn(nc, *args, out)
    result = run_bass_kernel_spmd(nc, [arrays], core_ids=[0])
    return result.results[0]["out"]
```

```python
from contextlib import ExitStack

import concourse.bass as bass
from concourse import mybir

F32 = mybir.dt.float32
BF16 = mybir.dt.bfloat16
F32R = mybir.dt.float32r
ALU = mybir.AluOpType
ACT = mybir.ActivationFunctionType
AX_X = mybir.AxisListType.X

P = 128
BANK = 512
EPS = 1e-5
HEADS = 16


class Chain:

    def __init__(self, engine, sem, done=0):
        self.engine, self.sem, self.done = engine, sem, done

    def __call__(self, instruction):
        self.done = self.done + 1
        instruction.then_inc(self.sem, 1)
        self.engine.wait_ge(self.sem, self.done)


def attention_and_butterfly_ffn(nc, x, w_qkv, b_qk_columns, b_v, w_exp, b_exp, up_planes, up_bias_columns, down_planes,
                                w_con_t, b_con, down_bias, out):
    B, N, D = x.shape
    HD = D // HEADS
    KD = D // P
    TILES = B * N // P
    CT = BANK // P
    CHUNKS = TILES // CT
    HID = w_exp.shape[1]
    HT = HID // P
    STAGES = up_planes.shape[0]
    PAIRS = HID // 2
    QB = 2048
    SUPER = B * N * HEADS // QB
    QG = QB // BANK
    QT = QB // P
    KT = N // P
    PARTS = 3
    ROWS = 6 * HD
    VW = 32
    REGIONS = QT * N // (2 * BANK)
    PER_KT = REGIONS // KT
    MAX_PARTS = 2
    AHEAD = 10
    BEHIND = 6

    q_dram = nc.dram_tensor("q_parts", [PARTS, B * D, N], BF16, kind="Internal").ap()
    k_dram = nc.dram_tensor("k_parts", [PARTS, B * D, N], BF16, kind="Internal").ap()
    v_dram = nc.dram_tensor("v_columns", [B * HEADS, P, KT, HD], F32, kind="Internal").ap()
    xnt_dram = nc.dram_tensor("xn_transposed", [P, KD, B * N], F32, kind="Internal").ap()

    x_tiles = x.rearrange("b (t p) d -> p (b t) d", p=P)
    out_tiles = out.rearrange("b (t p) d -> p (b t) d", p=P)

    with ExitStack() as ctx:
        before_ffn = ctx.enter_context(ExitStack())

        def sb(name, shape, dt=F32, until=ctx):
            return until.enter_context(nc.sbuf_tensor(name, shape, dt))

        def sem(name):
            return ctx.enter_context(nc.semaphore(name))

        psum = ctx.enter_context(nc.psum_tensor("psum", [P, 8, BANK], F32))
        y = sb("y", [P, TILES, D])
        ident = sb("ident", [P, P])
        ident_bf = sb("ident_bf", [P, P], BF16)
        one = sb("one", [1, 2])
        warm = sb("warm", [1, 2])
        w_up = sb("w_up", [P, 3, HID])
        w_down_t = sb("w_down_t", [P, KD, HID])
        planes = sb("planes", [P, 2, 4, PAIRS], until=before_ffn)
        fold = sb("fold", [P, 3, 3, PAIRS], until=before_ffn)

        arena = sb("arena", [P, 18432], until=before_ffn)
        at = [0]

        def take(shape, dt=F32):
            words = 1
            for n in shape[1:]:
                words *= n
            if dt == BF16:
                words //= 2
            ap = arena[0:shape[0], at[0]:at[0] + words]
            at[0] += words
            assert at[0] <= 18432
            if dt == BF16:
                ap = ap.bitcast(BF16)
            if len(shape) == 3:
                ap = ap.rearrange("p (a b) -> p a b", b=shape[2])
            if len(shape) == 4:
                ap = ap.rearrange("p (a b c) -> p a b c", b=shape[2], c=shape[3])
            return ap

        def row(vector, n=P):
            return vector.rearrange("(a d) -> a d", a=1).to_broadcast([n, vector.shape[0]])

        wqkv = take([P, KD, 3 * D])
        bqk = take([P, 2 * KD])
        bv = take([P, D])
        btail = take([P, 2, D])
        stats = take([P, 2 * CT, 6])
        mv = take([P, 2 * CT, 2])
        std = take([P, 2, CT])
        rstd = take([P, 2, CT])
        eps = take([P, 1])
        wait_slot = take([P, 1])
        xn = take([P, 2 * CT, D])
        xnt = take([P, 2 * KD, BANK])
        full = take([P, 2 * KD, BANK])
        rest = take([P, 2, BANK])
        v_sb = take([P, 2 * HEADS, CT * HD])
        parts = take([P, 2 * KD * PARTS, BANK], BF16)

        prepare_end = at[0]
        at[0] = 0
        probs = take([P, 4, QG * BANK])
        v_cols = take([P, 2 * KT, VW])
        q_rows = [take([P, QB], BF16) for _ in range(3)]
        k_rows = [take([P, N], BF16)]
        assert at[0] >= prepare_end
        k_rows.insert(0, take([P, N], BF16))
        q_rows.insert(0, take([P, QB], BF16))
        s_q = [sem(f"q_rows_loaded{n}") for n in range(4)]
        s_k = [sem(f"k_rows_loaded{n}") for n in range(2)]
        s_ones = sem("first_k_ones_set")
        LOADS = 3

        def load_q(sp, head, half, slot):
            for first, part, copies in ((0, 0, 3), (3, 1, 2), (5, 2, 1)):
                src = q_dram[part:part + 1, bass.ds(HD * head, HD), QB * half:QB * half + QB].to_broadcast([copies, HD, QB])
                sp.dma_start(q_rows[slot][HD * first:HD * (first + copies), :], src).then_inc(s_q[slot], 16)

        def load_k(sp, head, slot):
            for first, count in ((0, 3), (3, 2), (5, 1)):
                src = k_dram[0:count, bass.ds(HD * head, HD), :]
                sp.dma_start(k_rows[slot][HD * first:HD * (first + count), :], src).then_inc(s_k[slot], 16)

        ps_xt, ps_qk, ps_v = psum[:, 0:2, :], psum[:, 2:6, :], psum[:, 6:8, :]

        s_w = sem("weights_loaded")
        s_ident = sem("ident_made")
        s_x = [sem(f"x_loaded{n}") for n in range(2)]
        s_moments = sem("moments_done")
        s_std = sem("std_done")
        s_rstd = sem("rstd_done")
        s_xn = sem("xn_done")
        s_res = sem("residual_bias_added")
        s_xt_ps = sem("xt_transposed")
        s_xt = sem("xt_copied")
        s_qk_ps = sem("qk_multiplied")
        s_full = sem("qk_full_copied")
        s_high = sem("high_part_done")
        s_parts = sem("parts_done")
        s_v_ps = sem("v_multiplied")
        s_v = sem("v_done")
        s_dve = sem("dve_chain1")
        s_parts_out = [sem(f"parts_stored{n}") for n in range(2 * KD)]
        s_v_out = [sem(f"v_stored{n}") for n in range(2)]
        s_xt_out = [sem(f"xt_stored{n}") for n in range(2)]

        def chunk_loop(engine, step):
            for p in range(2):
                step(p, 0, p, p, CHUNKS - p)
            with engine.Fori(1, CHUNKS // 2 - 2) as i:
                for p in range(2):
                    step(2 * i + p, i, p, 2, CHUNKS)
            for c in range(CHUNKS - 4, CHUNKS):
                step(c, c // 2, c % 2, 2, CHUNKS - c)

        with nc.Block() as block:
            @block.gpsimd
            def _(pool):
                nc.gpsimd.memset(ident[:, :], 0.0).then_inc(s_ident, 1)
                nc.gpsimd.memset(ident_bf[:, :], 0.0).then_inc(s_ident, 1)
                nc.gpsimd.memset(one[:, :], 1.0).then_inc(s_ident, 1)
                nc.gpsimd.memset(eps, EPS).then_inc(s_ident, 1)
                pool.wait_ge(s_ident, 4)
                for m in (ident, ident_bf):
                    nc.gpsimd.affine_select(out=m[:, :], in_=m[:, :], compare_op=ALU.not_equal, fill=1.0,
                                            base=0, pattern=[[-1, P]], channel_multiplier=1).then_inc(s_ident, 1)
                pool.wait_ge(s_ident, 6)
                nc.gpsimd.memset(k_rows[0][ROWS:ROWS + MAX_PARTS, :], 1.0).then_inc(s_ones, 1)
                pool.wait_ge(s_ones, 1)
                pool.wait_ge(s_w, 16 * 5)
                nc.gpsimd.tensor_tensor(btail[:, 0, :], btail[:, 0, :], btail[:, 1, :], ALU.add).then_inc(s_res, 1)
                pool.wait_ge(s_res, 1)
                tail_bias = btail[:, 0, :].unsqueeze(1).to_broadcast([P, CT, D])
                with pool.Fori(0, CHUNKS) as c:
                    pool.wait_ge(s_xn, CT * c + CT)
                    tiles = y[:, bass.ds(CT * c, CT), :]
                    nc.gpsimd.tensor_tensor(tiles, tiles, tail_bias, ALU.add).then_inc(s_res, 1)

            @block.sync
            def _(sp):
                sp.dma_start(y[:, 0:CT, :], x_tiles[:, 0:CT, :]).then_inc(s_x[0], 16)
                sp.dma_start(y[:, CT:2 * CT, :], x_tiles[:, CT:2 * CT, :]).then_inc(s_x[1], 16)
                sp.dma_start(wqkv, w_qkv.rearrange("(k p) n -> p k n", p=P)).then_inc(s_w, 16)
                sp.dma_start(bqk, b_qk_columns).then_inc(s_w, 16)
                sp.dma_start(bv, row(b_v)).then_inc(s_w, 16)
                sp.dma_start(btail[:, 0, :], row(b_con)).then_inc(s_w, 16)
                sp.dma_start(btail[:, 1, :], row(down_bias)).then_inc(s_w, 16)
                for c in range(2, 4):
                    sp.wait_ge(s_moments, 2 * CT * (c - 1))
                    sp.dma_start(y[:, CT * c:CT * c + CT, :], x_tiles[:, CT * c:CT * c + CT, :]).then_inc(s_x[c % 2], 16)

                def step(c, i, p, before, left):
                    if left == 4:
                        for m in range(2 * KD):
                            sp.wait_ge(s_parts_out[m], 16 * (CHUNKS // B))
                        load_k(sp, 0, 0)
                        load_q(sp, 0, 0, 0)
                    if left > 4:
                        sp.wait_ge(s_moments, 2 * CT * (c + 3))
                        sp.dma_start(y[:, bass.ds(CT * c + 4 * CT, CT), :],
                                     x_tiles[:, bass.ds(CT * c + 4 * CT, CT), :]).then_inc(s_x[p], 16)
                    b, of_row = c // (CHUNKS // B), c % (CHUNKS // B)
                    sp.wait_ge(s_xt, KD * c + KD)
                    sp.dma_start(xnt_dram[:, :, bass.ds(BANK * c, BANK)], xnt[:, KD * p:KD * p + KD, :]).then_inc(s_xt_out[p], 16)
                    for m in range(2 * KD):
                        sp.wait_ge(s_parts, 2 * KD * c + m + 1)
                        rows = bass.ds(D * b + P * (m % KD), P)
                        dst = (q_dram if m < KD else k_dram)[:, rows, bass.ds(BANK * of_row, BANK)]
                        sp.dma_start(dst.rearrange("n r k -> r n k"), parts[:, PARTS * m:PARTS * m + PARTS, :])\
                          .then_inc(s_parts_out[m], 16)
                    sp.wait_ge(s_v, 2 * c + 2)
                    dst = v_dram[bass.ds(HEADS * b, HEADS), :, bass.ds(CT * of_row, CT), :].rearrange("h p t d -> p h (t d)")
                    sp.dma_start(dst, v_sb[:, HEADS * p:HEADS * p + HEADS, :]).then_inc(s_v_out[p], 16)

                chunk_loop(sp, step)
            @block.scalar
            def _(act):
                def deviation(c, p):
                    act.wait_ge(s_moments, 2 * CT * c + 2 * CT)
                    nc.scalar.activation(std[:, p, :], mv[:, CT * p:CT * p + CT, 1], ACT.Sqrt, bias=eps).then_inc(s_std, 1)

                act.wait_ge(s_ident, 6)
                nc.scalar.activation(warm[0:1, 0:1], one[0:1, 0:1], ACT.Sqrt)
                deviation(0, 0)
                deviation(1, 1)
                act.wait_ge(s_xt_ps, 1)
                for k in range(KD):
                    nc.scalar.copy(xnt[:, k, :], ps_xt[:, k, :]).then_inc(s_xt, 1)
                act.wait_ge(s_w, 16 * 5)

                def step(c, i, p, before, left):
                    def copy_next(q):
                        act.wait_ge(s_xt_ps, c + 2)
                        if before:
                            act.wait_ge(s_xt_out[q], 16 * (i + p))
                            act.wait_ge(s_v_ps, 2 * c)
                        for k in range(KD):
                            nc.scalar.copy(xnt[:, KD * q + k, :], ps_xt[:, k, :]).then_inc(s_xt, 1)

                    for m in range(2 * KD):
                        if m == KD and left > 1:
                            copy_next(1 - p)
                        act.wait_ge(s_qk_ps, 2 * KD * c + m + 1)
                        if before:
                            act.wait_ge(s_parts, 2 * KD * c)
                        dst, src = full[:, m, :], ps_qk[:, m, :]
                        if m < KD:
                            dst = dst.rearrange("p (t k) -> p k t", t=QT)
                            src = src.rearrange("p (k t) -> p k t", t=QT)
                        nc.scalar.activation(dst, src, ACT.Identity, bias=bqk[:, m:m + 1]).then_inc(s_full, 1)
                        act.wait_ge(s_full, 2 * KD * c + m + 1)
                        if before:
                            act.wait_ge(s_parts_out[m], 16 * c)
                        nc.scalar.copy(parts[:, PARTS * m, :], full[:, m, :]).then_inc(s_high, 1)
                    if left > 2:
                        deviation(c + 2, p)

                chunk_loop(act, step)

            @block.vector
            def _(dve):
                def x_tile(c, t):
                    return y[:, bass.ds(CT * c + t, 1), :].rearrange("p o d -> p (o d)")

                def moments(c, i, p, again=True):
                    dve.wait_ge(s_x[p], 16 * i + 16)
                    if again:
                        dve.wait_ge(s_xn, CT * c - CT)
                    for t in range(CT):
                        nc.vector.bn_stats(stats[:, CT * p + t, :], x_tile(c, t)).then_inc(s_moments, 1)
                    dve.wait_ge(s_moments, 2 * CT * c + CT)
                    nc.vector.memset(wait_slot, 0.0)
                    for t in range(CT):
                        nc.vector.bn_aggr(mv[:, CT * p + t, :], stats[:, CT * p + t, :]).then_inc(s_moments, 1)

                def normalise(c, p, again=True):
                    dve.wait_ge(s_std, c + 1)
                    if again:
                        dve.wait_ge(s_xt_ps, c - 1)
                    nc.vector.reciprocal(rstd[:, p, :], std[:, p, :]).then_inc(s_rstd, 1)
                    dve.wait_ge(s_rstd, c + 1)
                    for t in range(CT):
                        nc.vector.tensor_scalar(xn[:, CT * p + t, :], x_tile(c, t), mv[:, CT * p + t, 0:1],
                                                rstd[:, p, t:t + 1], ALU.subtract, ALU.mult).then_inc(s_xn, 1)

                for c in range(2):
                    moments(c, 0, c, again=False)
                    normalise(c, c, again=False)
                dve.wait_ge(s_w, 16 * 5)
                bv_pair = bv.unsqueeze(1).to_broadcast([P, 2, D]).rearrange("p t (h d) -> p t h d", d=HD)

                def split(c, m, before):
                    done = 2 * (2 * KD * c + m)
                    pair = range(2)
                    for q in pair:
                        dve.wait_ge(s_high, 2 * KD * c + m + q + 1)
                        if before or m:
                            dve.wait_ge(s_parts, 2 * KD * c + m + q - 1)
                        nc.vector.tensor_tensor(rest[:, q, :], full[:, m + q, :], parts[:, PARTS * (m + q), :],
                                                ALU.subtract).then_inc(s_dve, 1)
                    for q in pair:
                        dve.wait_ge(s_dve, done + q + 1)
                        nc.vector.tensor_copy(parts[:, PARTS * (m + q) + 1, :], rest[:, q, :]).then_inc(s_dve, 1)
                    for q in pair:
                        dve.wait_ge(s_dve, done + q + 3)
                        nc.vector.tensor_tensor(parts[:, PARTS * (m + q) + 2, :], rest[:, q, :],
                                                parts[:, PARTS * (m + q) + 1, :], ALU.subtract).then_inc(s_parts, 1)

                def step(c, i, p, before, left):
                    if left > 2:
                        moments(c + 2, i + 1, p)
                    split(c, 0, before)
                    if left > 2:
                        normalise(c + 2, p)
                    split(c, 2, before)
                    if before > 1:
                        dve.wait_ge(s_v_out[p], 16 * i)
                    for t in range(2):
                        dve.wait_ge(s_v_ps, 2 * c + t + 1)
                        dst = v_sb[:, HEADS * p:HEADS * p + HEADS, 2 * HD * t:2 * HD * t + 2 * HD]
                        nc.vector.tensor_tensor(dst.rearrange("p h (t d) -> p t h d", d=HD),
                                                ps_v[:, t, :].rearrange("p (t h d) -> p t h d", t=2, d=HD), bv_pair, ALU.add)\
                          .then_inc(s_v, 1)

                chunk_loop(dve, step)

            @block.tensor
            def _(pe):
                def transposes(c, p, first=False):
                    pe.wait_ge(s_xn, CT * c + CT)
                    if not first:
                        pe.wait_ge(s_xt, KD * c)
                    for k in range(KD):
                        for t in range(CT):
                            last = nc.tensor.transpose(ps_xt[:, k, P * t:P * t + P],
                                                       xn[:, CT * p + t, P * k:P * k + P], ident[:, :])
                    last.then_inc(s_xt_ps, 1)

                pe.wait_ge(s_ident, 6)
                transposes(0, 0, first=True)
                pe.wait_ge(s_w, 16 * 5)

                def step(c, i, p, before, left):
                    pe.wait_ge(s_xt, KD * c + KD)
                    if before:
                        pe.wait_ge(s_full, 2 * KD * c)
                    for m in range(2 * KD):
                        if m == KD and left > 1:
                            transposes(c + 1, 1 - p)
                        for k in range(KD):
                            last = nc.tensor.matmul(ps_qk[:, m, :], wqkv[:, k, P * m:P * m + P],
                                                    xnt[:, KD * p + k, :], start=(k == 0), stop=(k == KD - 1))
                        last.then_inc(s_qk_ps, 1)
                    if before:
                        pe.wait_ge(s_v, 2 * c)
                    for t in range(CT):
                        for k in range(KD):
                            last = nc.tensor.matmul(ps_v[:, t // 2, (t % 2) * D:(t % 2) * D + D],
                                                    xnt[:, KD * p + k, P * t:P * t + P],
                                                    wqkv[:, k, 2 * D:3 * D], start=(k == 0), stop=(k == KD - 1))
                        if t % 2:
                            last.then_inc(s_v_ps, 1)

                chunk_loop(pe, step)

        o_t = sb("o_t", [P, QT, VW], until=before_ffn)
        maxima = sb("maxima", [P, 2, REGIONS], until=before_ffn)
        neg_max = sb("neg_max", [P, QT], until=before_ffn)
        neg_parts = sb("neg_parts", [P, MAX_PARTS * QT], BF16, until=before_ffn)
        neg_rows = sb("neg_rows", [MAX_PARTS * QT, P], BF16, until=before_ffn)
        recip = sb("recip", [P, QT], until=before_ffn)

        ps_max = [psum[:, 0:2, :], psum[:, 2:4, :]]
        ps_s = psum[:, 4:7, :]
        ps_o = psum[:, 7, :]
        ps_neg = psum[0:MAX_PARTS * QT, 5, 0:P // 2].bitcast(BF16)
        WIDE_KT = (REGIONS - AHEAD) // PER_KT + 1

        def is_wide(c, kt, last):
            return last and (c == 3 or c == 2 and kt >= WIDE_KT)

        def score_bank(g, wide):
            return ps_max[0][:, 0, :] if wide and g == 2 else ps_s[:, (0, 1, 0, 2)[g], :]

        s_vc = [sem(f"v_cols_loaded{n}") for n in range(2)]
        s_set = sem("constants_set")
        s_region = sem("region_multiplied")
        s_region_free = sem("region_slot_free")
        s_fin = sem("maxima_finished")
        s_rows = sem("neg_rows_transposed")
        s_rows_sb = sem("neg_rows_copied")
        s_neg_in = sem("neg_rows_in_place")
        s_score = sem("scores_multiplied")
        s_exp = sem("exps_done")
        s_pv = sem("probs_used")
        s_o_free = sem("sums_transposed")
        s_evac = sem("sums_taken")
        s_plane = [sem(f"planes_loaded{n}") for n in range(2)]
        s_wld = sem("ffn_weights_loaded")
        s_fold = sem("pool_chain")
        ROWS_KT = (REGIONS - AHEAD) // PER_KT + 3
        FIN = 3
        EVAC = 3

        def superblocks(engine, step):
            with engine.Fori(0, SUPER // 4 - 1) as i:
                for c in range(4):
                    step(4 * i + c, c, i, False)
            i = SUPER // 4 - 1
            for c in range(4):
                step(4 * i + c, c, i, True)

        def wait_for_stores(engine):
            for m in range(2 * KD):
                engine.wait_ge(s_parts_out[m], 16 * CHUNKS)
            for p in range(2):
                engine.wait_ge(s_v_out[p], 16 * CHUNKS // 2)
                engine.wait_ge(s_xt_out[p], 16 * CHUNKS // 2)

        with nc.Block() as block:
            @block.gpsimd
            def _(pool):
                wait_for_stores(pool)
                ones = Chain(pool, s_set)
                ones(nc.gpsimd.memset(k_rows[1][ROWS:ROWS + MAX_PARTS, :], 1.0))
                ones(nc.gpsimd.memset(v_cols[:, :, HD:HD + 1], 1.0))
                ones(nc.gpsimd.memset(v_cols[:, :, HD + 1:VW], 0.0))
                chain = Chain(pool, s_fold)
                chain(nc.gpsimd.memset(w_up[:, 2, :], 0.0))
                pool.dma_start(w_up[:, 0:KD, :], w_exp.rearrange("(k p) n -> p k n", p=P)).then_inc(s_wld, 16)
                pool.dma_start(w_up[0:1, 2, :], row(b_exp, 1)).then_inc(s_wld, 16)
                pool.dma_start(w_down_t[:, :, :], w_con_t.rearrange("(k p) n -> p k n", p=P)).then_inc(s_wld, 16)
                pool.wait_ge(s_wld, 48)
                turns = [(w_up, 3, up_planes, s) for s in range(STAGES)]
                turns += [(w_down_t, KD, down_planes, s) for s in reversed(range(STAGES))]

                def load_planes(n):
                    _, _, src, s = turns[n]
                    flat = src[s].rearrange("a b k -> (a b k)")
                    pool.dma_start(planes[:, n % 2, :, :].rearrange("p a k -> p (a k)"), row(flat)).then_inc(s_plane[n % 2], 16)

                load_planes(0)
                for n, (w, rows, _, s) in enumerate(turns):
                    if n + 1 < len(turns):
                        load_planes(n + 1)
                    pool.wait_ge(s_plane[n % 2], 16 * (n // 2 + 1))
                    stride = 2 ** s
                    pair = w[:, :, :].rearrange("p r (n two s) -> p r n two s", two=2, s=stride)
                    down = w is w_down_t
                    for r in range(rows):
                        a, b = pair[:, r, :, 0, :], pair[:, r, :, 1, :]

                        def plane(to, of):
                            index = 2 * of + to if down else 2 * to + of
                            return planes[:, n % 2, index, :].rearrange("p (n s) -> p n s", s=stride)

                        def tmp(q):
                            return fold[:, r, q, :].rearrange("p (n s) -> p n s", s=stride)

                        mult, add = ALU.mult, ALU.add
                        nc.gpsimd.tensor_tensor(tmp(0), a, plane(0, 0), mult).then_inc(s_fold, 1)
                        nc.gpsimd.tensor_tensor(tmp(1), b, plane(0, 1), mult).then_inc(s_fold, 1)
                        chain.done += 2
                        chain(nc.gpsimd.tensor_tensor(tmp(2), a, plane(1, 0), mult))
                        chain(nc.gpsimd.tensor_tensor(a, tmp(0), tmp(1), add))
                        chain(nc.gpsimd.tensor_tensor(tmp(0), b, plane(1, 1), mult))
                        chain(nc.gpsimd.tensor_tensor(b, tmp(2), tmp(0), add))

            @block.sync
            def _(sp):
                def load_v(n, slot):
                    src = v_dram[bass.ds(n, 1), :, :, :].rearrange("o p t d -> (o p) t d")
                    sp.dma_start(v_cols[:, KT * slot:KT * slot + KT, 0:HD], src).then_inc(s_vc[slot], 16)

                def place_neg(n, slot):
                    sp.wait_ge(s_rows_sb, n + 1)
                    sp.dma_start(q_rows[slot][ROWS:ROWS + MAX_PARTS, :], neg_rows[:, :]).then_inc(s_neg_in, 16)

                wait_for_stores(sp)
                load_q(sp, 0, 1, 1)
                load_v(0, 0)
                place_neg(0, 0)

                def step(s, c, i, last):
                    head = 2 * i + c // 2 + 1
                    more = not (last and c >= 2)
                    sp.wait_ge(s_exp, KT * QG * s + 4)
                    if more:
                        load_q(sp, head, c % 2, (c + 2) % 4)
                    if more and c % 2 == 0:
                        load_k(sp, head, (c // 2 + 1) % 2)
                        sp.wait_ge(s_pv, KT * s + 4)
                        load_v(head, (c // 2 + 1) % 2)
                    if not (last and c == 3):
                        place_neg(s + 1, (c + 1) % 4)

                superblocks(sp, step)
                sp.wait_ge(s_neg_in, 16 * SUPER)
                for n in range(4):
                    sp.wait_ge(s_q[n], 16 * LOADS * SUPER // 4)
                for n in range(2):
                    sp.wait_ge(s_k[n], 16 * LOADS * SUPER // 4)
                    sp.wait_ge(s_vc[n], 16 * SUPER // 4)

            @block.scalar
            def _(act):
                def step(s, c, i, last):
                    for kt in range(KT):
                        act.wait_ge(s_pv, KT * s + kt + 1)
                        for g in range(QG):
                            act.wait_ge(s_score, QG * (KT * s + kt) + g + 1)
                            nc.scalar.activation(probs[:, kt % 4, BANK * g:BANK * g + BANK],
                                                 score_bank(g, is_wide(c, kt, last)), ACT.Exp).then_inc(s_exp, 1)

                superblocks(act, step)

            @block.vector
            def _(dve):
                for n, (signal, count) in enumerate(((s_region_free, 2), (s_exp, 4), (s_pv, 4), (s_o_free, 1), (s_evac, 1))):
                    nc.vector.memset(recip[:, n:n + 1], 0.0).then_inc(signal, count)

                def reduce_region(m, n, parity):
                    dve.wait_ge(s_region, REGIONS * m + n + 1)
                    nc.vector.tensor_reduce(maxima[:, parity, n:n + 1], ps_max[n % 2].rearrange("p a b -> p (a b)"),
                                            axis=AX_X, op=ALU.max).then_inc(s_region_free, 1)

                def finish_maxima(m, parity, first=False):
                    high, low = neg_parts[:, 0:QT], neg_parts[:, QT:2 * QT]

                    def negate():
                        dve.wait_ge(s_region_free, REGIONS * m + REGIONS + 2)
                        nc.vector.tensor_reduce(neg_max[:, :], maxima[:, parity, :].rearrange("p (t r) -> p t r", t=QT),
                                                axis=AX_X, op=ALU.max, negate=True).then_inc(s_fin, 1)

                    def high_part():
                        dve.wait_ge(s_fin, FIN * m + 1)
                        nc.vector.tensor_copy(high, neg_max[:, :]).then_inc(s_fin, 1)

                    def low_part():
                        dve.wait_ge(s_fin, FIN * m + 2)
                        nc.vector.tensor_tensor(low, neg_max[:, :], high, ALU.subtract).then_inc(s_fin, 1)

                    def copy_rows():
                        if not first:
                            dve.wait_ge(s_neg_in, 16 * m)
                        dve.wait_ge(s_rows, m + 1)
                        nc.vector.tensor_copy(neg_rows[:, :], ps_neg).then_inc(s_rows_sb, 1)

                    return [negate, high_part, low_part, copy_rows]

                def take_sums(s):
                    dims = o_t[:, :, 0:HD]
                    dst = y[:, bass.ds(s, 1), :].rearrange("p o (t d) -> p (o t) d", d=HD)

                    def turn():
                        dve.wait_ge(s_pv, KT * s + KT + 4)
                        dve.wait_ge(s_evac, EVAC * s + 1)
                        nc.vector.transpose(o_t[:, :, :].rearrange("p t v -> p (t v)"), ps_o).then_inc(s_o_free, 1)

                    def invert():
                        dve.wait_ge(s_o_free, s + 2)
                        nc.vector.reciprocal(recip[:, :], o_t[:, :, HD]).then_inc(s_evac, 1)

                    def scale():
                        dve.wait_ge(s_evac, EVAC * s + 2)
                        nc.vector.tensor_tensor(dims, dims, recip[:, :].unsqueeze(2).to_broadcast([P, QT, HD]), ALU.mult)\
                          .then_inc(s_evac, 1)

                    def add():
                        dve.wait_ge(s_evac, EVAC * s + 3)
                        nc.vector.tensor_tensor(dst, dst, dims, ALU.add).then_inc(s_evac, 1)

                    return [turn, invert, scale, add]

                for n in range(REGIONS):
                    reduce_region(0, n, 0)
                for f in finish_maxima(0, 0, first=True):
                    f()
                for n in range(AHEAD + BEHIND):
                    reduce_region(1, n, 1)

                def step(s, c, i, last):
                    after = {}
                    for q, f in enumerate(finish_maxima(s + 1, (c + 1) % 2)):
                        after[REGIONS - AHEAD - BEHIND - 1 + PER_KT * q] = f
                    for q, f in enumerate(take_sums(s)):
                        after[REGIONS - BEHIND + PER_KT * q - 1] = f
                    for r in range(REGIONS):
                        m, n = divmod(AHEAD + BEHIND + r, REGIONS)
                        m += c + 1 - 4 * (last is True)
                        if not last or m < 0:
                            reduce_region(m + (4 * i if not last else SUPER), n, m % 2)
                        if r in after and not (last and c == 3 and r < REGIONS - BEHIND - 1):
                            after[r]()

                superblocks(dve, step)

            @block.tensor
            def _(pe):
                def region_half(m, c, n, half):
                    if half == 0:
                        pe.wait_ge(s_region_free, REGIONS * m + n + 1)
                    t, keys = n // 4, (n % 4 * 2 + half) * BANK
                    mm = nc.tensor.matmul(ps_max[n % 2][:, half, :], q_rows[c][0:ROWS, P * t:P * t + P],
                                          k_rows[c // 2][0:ROWS, keys:keys + BANK], start=True, stop=True)
                    if half == 1:
                        mm.then_inc(s_region, 1)

                def neg_to_rows(m, exps):
                    pe.wait_ge(s_fin, FIN * (m + 1))
                    pe.wait_ge(s_exp, exps + 4)
                    nc.tensor.transpose(ps_neg, neg_parts[:, :], ident_bf[:, :]).then_inc(s_rows, 1)

                def scores(s, c, kt, g, wide=False, rows=None):
                    first = isinstance(s, int) and s == 0
                    if kt == 0 and g == 0:
                        pe.wait_ge(s_neg_in, 16 * (s + 1))
                    if rows is not None:
                        pe.wait_ge(s_rows_sb, rows + 1)
                    if not first:
                        back = 2 if g % 2 == 0 and not wide else 4
                        pe.wait_ge(s_exp, QG * (KT * s + kt) + g + 5 - back)
                    nc.tensor.matmul(score_bank(g, wide), k_rows[c // 2][0:ROWS + MAX_PARTS, P * kt:P * kt + P],
                                     q_rows[c][0:ROWS + MAX_PARTS, BANK * g:BANK * g + BANK],
                                     start=True, stop=True).then_inc(s_score, 1)

                def sums(s, c, kt):
                    if kt == 0:
                        pe.wait_ge(s_o_free, s + 1)
                    pe.wait_ge(s_exp, QG * (KT * s + kt + 1) + 4)
                    for g in range(QG):
                        last = nc.tensor.matmul(ps_o[VW * g:VW * g + VW, :], v_cols[:, KT * (c // 2) + kt, :],
                                                probs[:, kt % 4, BANK * g:BANK * g + BANK],
                                                start=(kt == 0), stop=(kt == KT - 1))
                    last.then_inc(s_pv, 1)

                pe.wait_ge(s_k[0], 16 * LOADS)
                pe.wait_ge(s_q[0], 16 * LOADS)
                for n in range(REGIONS):
                    region_half(0, 0, n, 0)
                    region_half(0, 0, n, 1)
                pe.wait_ge(s_fin, FIN)
                nc.tensor.transpose(ps_neg, neg_parts[:, :], ident_bf[:, :]).then_inc(s_rows, 1)
                pe.wait_ge(s_q[1], 16 * LOADS)
                for n in range(AHEAD):
                    region_half(1, 1, n, 0)
                    region_half(1, 1, n, 1)
                pe.wait_ge(s_ones, 1)
                pe.wait_ge(s_set, 3)
                scores(0, 0, 0, 0)
                scores(0, 0, 0, 1, rows=0)

                def step(s, c, i, last):
                    if c % 2 == 0:
                        pe.wait_ge(s_vc[c // 2], 16 * (i + 1))
                    for kt in range(KT):
                        halves = []
                        for n in range(PER_KT):
                            d, n = divmod(AHEAD + PER_KT * kt + n, REGIONS)
                            to = c + 1 + d
                            if last and to >= 4:
                                continue
                            if d == 1 and n == 0:
                                pe.wait_ge(s_q[to % 4], 16 * LOADS * (i + 1 + to // 4))
                                pe.wait_ge(s_k[to // 2 % 2], 16 * LOADS * (i + 1 + to // 4))
                            halves += [(4 * i + to, to % 4, n, h) for h in range(2)]
                        more = not (last and c == 3)
                        rows = s + 1 if kt == ROWS_KT and more else None
                        if rows is not None:
                            neg_to_rows(rows, QG * (KT * s + kt) + 2)
                        s1, c1, kt1 = (s, c, kt + 1) if kt < KT - 1 else (s + 1, (c + 1) % 4, 0)
                        if kt1 or more:
                            wide = is_wide(c1, kt1, last)
                        if not is_wide(c, kt, last):
                            scores(s, c, kt, 2)
                            for h in halves[0:1]:
                                region_half(*h)
                            scores(s, c, kt, 3)
                            for h in halves[1:3]:
                                region_half(*h)
                        if kt1 or more:
                            scores(s1, c1, kt1, 0, wide and is_wide(c, kt, last))
                            for h in halves[3:4]:
                                region_half(*h)
                            scores(s1, c1, kt1, 1, wide, rows)
                            if wide:
                                if not is_wide(c, kt, last):
                                    pe.wait_ge(s_region_free, REGIONS * SUPER + 2)
                                scores(s1, c1, kt1, 2, wide)
                                scores(s1, c1, kt1, 3, wide)
                        sums(s, c, kt)

                superblocks(pe, step)

        before_ffn.close()
        xnt2 = sb("xnt2", [P, 2 * KD, BANK])
        xn_high = sb("xn_high", [P, 2 * KD, BANK], F32R)
        xn_low = sb("xn_low", [P, 2 * KD, BANK], F32R)
        gelus = sb("gelus", [P, 2, BANK])
        hidden_high = sb("hidden_high", [P, HT, BANK], F32R)
        hidden_low = sb("hidden_low", [P, HT, BANK], F32R)
        w_up_high = sb("w_up_high", [P, KD, HID], F32R)
        w_up_low = sb("w_up_low", [P, KD, HID], F32R)
        w_down_high = sb("w_down_high", [P, HT, D], F32R)
        w_down_low = sb("w_down_low", [P, HT, D], F32R)
        bias_up = sb("bias_up", [P, 2, HT])

        ps_h = psum[:, 0:4, :]
        ps_d = psum[:, 4:8, :]

        s_bup = sem("up_bias_loaded")
        s_wt_ps = sem("w_down_transposed")
        s_wt_high = sem("w_down_high_parts")
        s_wt = sem("w_down_split")
        s_wu_high = sem("w_up_high_parts")
        s_wu = sem("w_up_split")
        s_xp_high = sem("xn_high_parts")
        s_xp = sem("xn_split")
        s_bias_ps = sem("bias_row_turned")
        s_bias = sem("bias_added")
        s_xnt2 = [sem(f"xn_transposed_loaded{n}") for n in range(2)]
        s_h_ps = sem("hidden_multiplied")
        s_h = sem("gelu_done")
        s_h_high = sem("hidden_high_parts")
        s_h_low = sem("hidden_split")
        s_d_ps = sem("down_multiplied")
        s_d = sem("down_added")
        s_out = sem("out_stored")

        def ffn_loop(engine, step):
            for p in range(2):
                step(p, 0, p, p == 0)
            with engine.Fori(1, CHUNKS // 2) as i:
                for p in range(2):
                    step(2 * i + p, i, p, False)

        with nc.Block() as block:
            @block.sync
            def _(sp):
                sp.dma_start(bias_up[:, 0, :], up_bias_columns).then_inc(s_bup, 16)

                def load(c, p):
                    sp.dma_start(xnt2[:, KD * p:KD * p + KD, :], xnt_dram[:, :, bass.ds(BANK * c, BANK)]).then_inc(s_xnt2[p], 16)

                load(0, 0)
                load(1, 1)

                def step(c, p, more=True):
                    if more:
                        sp.wait_ge(s_xp, c + 1)
                        load(c + 2, p)
                    sp.wait_ge(s_d, c + 1)
                    tiles = bass.ds(CT * c, CT)
                    sp.dma_start(out_tiles[:, tiles, :], y[:, tiles, :]).then_inc(s_out, 16)

                with sp.Fori(0, CHUNKS // 2 - 1) as i:
                    for p in range(2):
                        step(2 * i + p, p)
                for p in range(2):
                    step(CHUNKS - 2 + p, p, more=False)
                sp.wait_ge(s_out, 16 * CHUNKS)
                for p in range(2):
                    sp.wait_ge(s_xnt2[p], 16 * CHUNKS // 2)

            @block.tensor
            def _(pe):
                for m in range(HT):
                    if m == 4:
                        for n in range(HT):
                            last = nc.tensor.matmul(ps_d[:, 0, n:n + 1], w_up[0:1, 2, P * n:P * n + P], one[0:1, 0:1],
                                                    start=True, stop=True)
                        last.then_inc(s_bias_ps, 1)
                    if m >= 4:
                        pe.wait_ge(s_wt, m - 3)
                    for k in range(KD):
                        last = nc.tensor.transpose(ps_h[:, m % 4, P * k:P * k + P],
                                                   w_down_t[:, k, P * m:P * m + P], ident[:, :])
                    last.then_inc(s_wt_ps, 1)
                pe.wait_ge(s_wt, HT)
                pe.wait_ge(s_wu, KD)
                pe.wait_ge(s_bias, 1)

                def up(c, i, p, first):
                    pe.wait_ge(s_xp, c + 1)
                    for m in range(HT):
                        if m >= 4:
                            pe.wait_ge(s_h, HT * c + m - 3)
                        elif not first:
                            pe.wait_ge(s_h, HT * c)
                        passes = [(w, x, k) for k in range(KD)
                                  for w, x in ((w_up_high, xn_high), (w_up_low, xn_high), (w_up_high, xn_low))]
                        for n, (w, x, k) in enumerate(passes):
                            last = nc.tensor.matmul(ps_h[:, m % 4, :], w[:, k, P * m:P * m + P], x[:, KD * p + k, :],
                                                    start=(n == 0), stop=(n == len(passes) - 1))
                        last.then_inc(s_h_ps, 1)

                def down(c, p, first):
                    if not first:
                        pe.wait_ge(s_d, c)
                    for m in range(HT):
                        pe.wait_ge(s_h_low, HT * c + m + 1)
                        for t in range(CT):
                            for n, (h, w) in enumerate(((hidden_high, w_down_high), (hidden_low, w_down_high),
                                                        (hidden_high, w_down_low))):
                                last = nc.tensor.matmul(ps_d[:, t, 0:D], h[:, m, P * t:P * t + P], w[:, m, :],
                                                        start=(m == 0 and n == 0), stop=(m == HT - 1 and n == 2))
                    last.then_inc(s_d_ps, 1)

                def step(c, i, p, first):
                    up(c, i, p, first)
                    down(c, p, first)

                ffn_loop(pe, step)

            @block.scalar
            def _(act):
                for k in range(KD):
                    nc.scalar.copy(w_up_high[:, k, :], w_up[:, k, :]).then_inc(s_wu_high, 1)
                nc.scalar.activation(warm[0:1, 1:2], one[0:1, 0:1], ACT.Gelu)
                act.wait_ge(s_bias, 1)

                def step(c, i, p, first):
                    for m in range(HT):
                        act.wait_ge(s_h_ps, HT * c + m + 1)
                        if not first or m >= 2:
                            act.wait_ge(s_h_low, HT * c + m - 1)
                        nc.scalar.activation(gelus[:, m % 2, :], ps_h[:, m % 4, :], ACT.Gelu,
                                             bias=bias_up[:, 1, m:m + 1]).then_inc(s_h, 1)
                        act.wait_ge(s_h, HT * c + m + 1)
                        nc.scalar.copy(hidden_high[:, m, :], gelus[:, m % 2, :]).then_inc(s_h_high, 1)

                ffn_loop(act, step)

            @block.vector
            def _(dve):
                def split_xn(c, i, p):
                    slot = slice(KD * p, KD * p + KD)
                    dve.wait_ge(s_xnt2[p], 16 * (i + 1))
                    nc.vector.tensor_copy(xn_high[:, slot, :], xnt2[:, slot, :]).then_inc(s_xp_high, 1)
                    dve.wait_ge(s_xp_high, c + 1)
                    nc.vector.tensor_tensor(xn_low[:, slot, :], xnt2[:, slot, :], xn_high[:, slot, :].bitcast(F32),
                                            ALU.subtract).then_inc(s_xp, 1)

                def w_down_high_part(m):
                    dve.wait_ge(s_wt_ps, m + 1)
                    nc.vector.tensor_copy(w_down_high[:, m, :], ps_h[:, m % 4, 0:D]).then_inc(s_wt_high, 1)

                w_down_high_part(0)
                for m in range(HT):
                    if m % 4 < 3:
                        w_down_high_part(m + 1)
                    dve.wait_ge(s_wt_high, m + 1)
                    nc.vector.tensor_tensor(w_down_low[:, m, :], ps_h[:, m % 4, 0:D], w_down_high[:, m, :].bitcast(F32),
                                            ALU.subtract).then_inc(s_wt, 1)
                    if m == 3:
                        w_down_high_part(4)
                for k in range(KD):
                    dve.wait_ge(s_wu_high, k + 1)
                    nc.vector.tensor_tensor(w_up_low[:, k, :], w_up[:, k, :], w_up_high[:, k, :].bitcast(F32),
                                            ALU.subtract).then_inc(s_wu, 1)
                split_xn(0, 0, 0)
                dve.wait_ge(s_bup, 16)
                dve.wait_ge(s_bias_ps, 1)
                nc.vector.tensor_tensor(bias_up[:, 1, :], bias_up[:, 0, :], ps_d[:, 0, 0:HT], ALU.add).then_inc(s_bias, 1)

                def step(c, i, p, left):
                    for m in range(HT):
                        dve.wait_ge(s_h_high, HT * c + m + 1)
                        nc.vector.tensor_tensor(hidden_low[:, m, :], gelus[:, m % 2, :], hidden_high[:, m, :].bitcast(F32),
                                                ALU.subtract).then_inc(s_h_low, 1)
                    if left > 1:
                        split_xn(c + 1, i + p, 1 - p)
                    dve.wait_ge(s_d_ps, c + 1)
                    tiles = y[:, bass.ds(CT * c, CT), :]
                    nc.vector.tensor_tensor(tiles, ps_d[:, :, 0:D], tiles, ALU.add).then_inc(s_d, 1)

                with dve.Fori(0, CHUNKS // 2 - 1) as i:
                    for p in range(2):
                        step(2 * i + p, i, p, 2)
                for p in range(2):
                    step(CHUNKS - 2 + p, CHUNKS // 2 - 1, p, 2 - p)


def kernel(L0_attn_x, L0_attn_W_qkv, L0_attn_b_qkv, L0_ffn_W_exp, L0_ffn_b_exp, L0_ffn_up_weights, L0_ffn_up_bias,
           L0_ffn_down_weights, L0_ffn_W_con, L0_ffn_b_con, L0_ffn_down_bias):
    import numpy as np
    import concourse.bacc as bacc
    from concourse.bass_utils import run_bass_kernel_spmd

    def planes(weights):
        return np.ascontiguousarray(np.asarray(weights).transpose(0, 2, 3, 1))

    def columns(vector):
        return np.asarray(vector).reshape(-1, P).T

    D = L0_attn_x.shape[-1]
    data = {
        "x": np.asarray(L0_attn_x), "w_qkv": np.asarray(L0_attn_W_qkv), "b_qk_columns": columns(L0_attn_b_qkv[:2 * D]),
        "b_v": np.asarray(L0_attn_b_qkv[2 * D:]),
        "w_exp": np.asarray(L0_ffn_W_exp), "b_exp": np.asarray(L0_ffn_b_exp),
        "up_planes": planes(L0_ffn_up_weights), "up_bias_columns": columns(L0_ffn_up_bias),
        "down_planes": planes(L0_ffn_down_weights),
        "w_con_t": np.ascontiguousarray(np.asarray(L0_ffn_W_con).transpose(1, 0)),
        "b_con": np.asarray(L0_ffn_b_con), "down_bias": np.asarray(L0_ffn_down_bias),
    }
    nc = bacc.Bacc("TRN2", target_bir_lowering=False, num_devices=1)
    arrays, args = {}, []
    for name, a in data.items():
        a = np.ascontiguousarray(a)
        arrays[f"in_{name}"] = a
        args.append(nc.dram_tensor(f"in_{name}", a.shape, mybir.dt.from_np(a.dtype), kind="ExternalInput").ap())
    shape = data["x"].shape
    out = nc.dram_tensor("out", shape, F32, kind="ExternalOutput").ap()
    attention_and_butterfly_ffn(nc, *args, out)
    result = run_bass_kernel_spmd(nc, [arrays], core_ids=[0])
    return result.results[0]["out"]
```
